# Optimizing a Trainium2 kernel written in Bass

```python
import numpy as np
import jax
import jax.numpy as jnp

def _softmax(x, axis=-1):
    return jax.nn.softmax(x, axis=axis)

def _gelu(x):
    return jax.nn.gelu(x, approximate=True)

def _silu(x):
    return jax.nn.silu(x)

def _sigmoid(x):
    return jax.nn.sigmoid(x)

def _layernorm(x, axis=-1, eps=1e-05):
    m = jnp.mean(x, axis=axis, keepdims=True)
    v = jnp.var(x, axis=axis, keepdims=True)
    return (x - m) / jnp.sqrt(v + eps)

def _scatter_add(tgt, idx, src, axis=0):
    return tgt.at[idx].add(src)

def _segment_sum(src, seg, n):
    return jax.ops.segment_sum(src, seg, n)
kernel_name = 'mk_xattn_seq_d1_seqx_r8_1af5b7'

def setup_inputs(seed: int=0):
    np.random.seed(seed)
    _w = jnp.asarray

    def _rec_inputs():
        import jax
        import jax.numpy as jnp
        _rk = jax.random.key(seed)
        x = -0.0002928 + 1 * jax.random.normal(jax.random.fold_in(_rk, 1), (16, 100, 128), jnp.float32)
        _lenS = 100 - jax.random.randint(jax.random.fold_in(_rk, 7), (16,), 0, max(1, 100 // 4) + 1, jnp.int32)
        _lenS2 = 1444 - jax.random.randint(jax.random.fold_in(_rk, 8), (16,), 0, max(1, 1444 // 4) + 1, jnp.int32)
        _ctx_1024P = jax.random.normal(jax.random.fold_in(_rk, 11), (16, 16, 128), jnp.float32)
        _ctx_1024c = jax.random.dirichlet(jax.random.fold_in(_rk, 511), 0.3 * jnp.ones((16,), jnp.float32), (16, 1444))
        _ctx_1024t = jnp.einsum('bsk,bkd->bsd', _ctx_1024c, _ctx_1024P)
        _ctx_1024t = _ctx_1024t * jax.lax.rsqrt(jnp.mean(jnp.square(_ctx_1024t)) + 1e-12) * 0.953939
        ctx_1024 = -1.39393e-06 + 0.999914 * (_ctx_1024t + 0.3 * jax.random.normal(jax.random.fold_in(_rk, 611), (16, 1444, 128), jnp.float32))
        return (x, ctx_1024)
    x, ctx_1024 = _rec_inputs()

    def _L0_xattn_setup():
        import jax, jax.numpy as jnp
        import numpy as np
        NUM_HEADS = 16
        NEG = jnp.float32(-2 ** 32 + 1)
        key = jax.random.key(seed)
        ks = jax.random.split(key, 6)
        B, S, D = (2, 256, 128)
        init = (2.0 / (D + D)) ** 0.5
        return {'queries': jax.random.normal(ks[0], (B, S, D), jnp.float32), 'keys': jax.random.normal(ks[1], (B, S, D), jnp.float32), 'values': jax.random.normal(ks[2], (B, S, D), jnp.float32), 'Wq': jax.random.normal(ks[3], (D, D), jnp.float32) * init, 'bq': jnp.zeros((D,), jnp.float32), 'Wk': jax.random.normal(ks[4], (D, D), jnp.float32) * init, 'bk': jnp.zeros((D,), jnp.float32), 'Wv': jax.random.normal(ks[5], (D, D), jnp.float32) * init, 'bv': jnp.zeros((D,), jnp.float32)}
    _L0_xattn_all = _L0_xattn_setup()
    _L0_xattn_in = {k: v for k, v in _L0_xattn_all.items() if k in ('Wq', 'bq', 'Wk', 'bk', 'Wv', 'bv')}
    del _L0_xattn_all
    return {'x': x, 'ctx_1024': ctx_1024, 'L0_xattn_Wq': _L0_xattn_in['Wq'], 'L0_xattn_bq': _L0_xattn_in['bq'], 'L0_xattn_Wk': _L0_xattn_in['Wk'], 'L0_xattn_bk': _L0_xattn_in['bk'], 'L0_xattn_Wv': _L0_xattn_in['Wv'], 'L0_xattn_bv': _L0_xattn_in['bv']}

def reference(x, ctx_1024, L0_xattn_Wq, L0_xattn_bq, L0_xattn_Wk, L0_xattn_bk, L0_xattn_Wv, L0_xattn_bv):
    import jax
    import jax.numpy as jnp

    def _L0_xattn_ref(queries, keys, values, Wq, bq, Wk, bk, Wv, bv):
        import jax, jax.numpy as jnp
        import numpy as np
        NUM_HEADS = 16
        NEG = jnp.float32(-2 ** 32 + 1)
        H = NUM_HEADS
        B, Sq, D = queries.shape
        Sk = keys.shape[1]
        dh = D // H
        Q = jax.nn.relu(queries @ Wq + bq)
        K = jax.nn.relu(keys @ Wk + bk)
        V = jax.nn.relu(values @ Wv + bv)
        Qh = Q.reshape(B, Sq, H, dh).transpose(2, 0, 1, 3)
        Kh = K.reshape(B, Sk, H, dh).transpose(2, 0, 1, 3)
        Vh = V.reshape(B, Sk, H, dh).transpose(2, 0, 1, 3)
        scale = jnp.float32(1.0 / dh ** 0.5)
        scores = jnp.einsum('hbqd,hbkd->hbqk', Qh, Kh) * scale
        key_mask = jnp.sign(jnp.abs(jnp.sum(jax.lax.stop_gradient(keys), axis=-1)))
        scores = jnp.where(key_mask[None, :, None, :] == 0.0, NEG, scores)
        attn = jax.nn.softmax(scores, axis=-1)
        q_mask = jnp.sign(jnp.abs(jnp.sum(jax.lax.stop_gradient(queries), axis=-1)))
        attn = attn * q_mask[None, :, :, None]
        out = jnp.einsum('hbqk,hbkd->hbqd', attn, Vh)
        out = out.transpose(1, 2, 0, 3).reshape(B, Sq, D)
        return out + queries
    x = _L0_xattn_ref(x, ctx_1024, ctx_1024, L0_xattn_Wq, L0_xattn_bq, L0_xattn_Wk, L0_xattn_bk, L0_xattn_Wv, L0_xattn_bv)
    return x

_drawn_inputs = setup_inputs


def setup_inputs(seed=0):
    import zlib

    import numpy as np

    out = dict(_drawn_inputs(seed))
    spreads = {'L0_xattn_bq': (0.0, 0.8), 'L0_xattn_bk': (0.0, 2.0), 'L0_xattn_bv': (0.0, 0.1)}
    factors = {}
    for name, (base, spread) in spreads.items():
        noise = np.random.default_rng([zlib.crc32(name.encode()), seed]).standard_normal(out[name].shape)
        drawn = base * np.exp(spread * noise) if base else spread * noise
        out[name] = jnp.asarray(drawn.astype(out[name].dtype))
    for name, factor in factors.items():
        out[name] = (out[name] * factor).astype(out[name].dtype)
    return out
```

```python
from contextlib import ExitStack

import concourse.bass as bass
from concourse import mybir

F32 = mybir.dt.float32
F32R = mybir.dt.float32r
I32 = mybir.dt.int32
ALU = mybir.AluOpType
ACT = mybir.ActivationFunctionType
AX = mybir.AxisListType

P = 128
BANK = 512

SLOTS = 4
HEADS = 16
QUAD = 4
PAIR = 2
VCOLS = 32
SCORE_SLOTS = 3
PROB_SLOTS = 4
LEAD = 2
SHIFT = 40.0
BOUND_LIMIT = 100.0
DEN_FLOOR = 1e-30
NEG = float(2 ** 32)


def attention(
    nc: bass.Bass,
    x: bass.AP,
    xT: bass.AP,
    ctxT: bass.AP,
    Wq: bass.AP,
    bq: bass.AP,
    Wk: bass.AP,
    bk: bass.AP,
    Wv: bass.AP,
    bv: bass.AP,
    out: bass.AP,
):
    B, SQ, D = x.shape
    SK = ctxT.shape[2]
    DH = D // HEADS
    SCALE = 1.0 / DH ** 0.5
    KT = -(-SK // P)
    SKP = KT * P
    QUADS = HEADS // QUAD
    PAIRS = HEADS // PAIR
    HALVES = 2
    HALF_PAIRS = PAIRS // HALVES
    HALF_QUADS = QUADS // HALVES
    UNITS = KT * HALVES
    QCOLS = QUAD * SQ
    PCOLS = PAIR * SQ
    VW = D + 1
    VGROUP = 3
    VGROUPS = KT // VGROUP
    KCHUNKS = SKP // BANK
    QB = 4
    assert D == P and DH * QUAD == 32 and VGROUP * VW <= BANK and HALF_PAIRS * VCOLS == P
    assert UNITS % SCORE_SLOTS == 0 and UNITS % PROB_SLOTS == 0 and B % 2 == 0 and B % QB == 0
    assert QB * SQ <= BANK and QCOLS <= BANK and HALVES * PCOLS <= BANK
    REPLICAS = SLOTS * QUADS

    ctx = ExitStack()
    with ctx:
        def sb(name, shape, dt=F32):
            return ctx.enter_context(nc.sbuf_tensor(name, shape, dt))

        def sem(name):
            return ctx.enter_context(nc.semaphore(name))

        wq_sb = sb("wq_sb", [P, D])
        wk_sb = sb("wk_sb", [P, D])
        wv_sb = sb("wv_sb", [P, VW])
        bq_sb = sb("bq_sb", [P, 1])
        bk_sb = sb("bk_sb", [P, 1])
        bv_sb = sb("bv_sb", [P, D])
        ident = sb("ident", [P, P])
        blockmask = sb("blockmask", [P, QUAD])
        shift_sb = sb("shift_sb", [P, 1])
        keyT = sb("keyT", [P, 2, SKP])
        queryT = sb("queryT", [P, B * SQ])
        query_rep = sb("query_rep", [P, QUADS, B * SQ], F32R)
        query_bd = sb("query_bd", [P, 2, QUADS, QCOLS], F32R)
        k_raw = sb("k_raw", [P, SKP])
        k_cent = sb("k_cent", [P, SKP])
        k_high = sb("k_high", [P, SKP], F32R)
        k_low = sb("k_low", [P, SKP], F32R)
        k_parts = sb("k_parts", [P, 2, QUADS, SKP], F32R)
        k_chunk_max = sb("k_chunk_max", [P, KCHUNKS + 1])
        k_max = sb("k_max", [P, 2])
        v_biased = sb("v_biased", [P, 2, VGROUP, D])
        keep = sb("keep", [P, KT])
        values = sb("values", [P, 2, KT, PAIRS, VCOLS])
        probs = sb("probs", [P, PROB_SLOTS, HALF_QUADS, QCOLS])
        o_sb = sb("o_sb", [P, HALVES * PCOLS])
        inv_den = sb("inv_den", [SQ, HALVES * PAIR, HALF_PAIRS])
        o_norm = sb("o_norm", [SQ, D])
        x_sb = sb("x_sb", [SQ, B, D])
        q_sum = sb("q_sum", [SQ, B])
        q_mask = sb("q_mask", [SQ, B])
        out_sb = sb("out_sb", [SQ, B, D])
        q_max = sb("q_max", [P, B])

        head_sum = sb("head_sum", [P, HEADS])
        ones = sb("ones", [P, P])
        bound_terms = sb("bound_terms", [P, B])
        kept_keys = sb("kept_keys", [P, B])
        batch_checks = sb("batch_checks", [B, 4])
        bounded = sb("bounded", [1, 1], I32)

        g_keys = k_raw
        g_keep = k_cent
        g_values = values[:, 0].rearrange("p a b c -> p (a b c)")[:, 0:KT * D].rearrange("p (n w) -> p n w", w=D)
        g_mask = probs[:].rearrange("p a b c -> p (a b c)")[:, 0:SKP]
        g_scores = probs[:].rearrange("p a b c -> p (a b c)")[0:SQ, SKP:2 * SKP]
        g_probsT = values[:, 1].rearrange("p a b c -> p (a b c)")[:, 0:KT * P].rearrange("p (n q) -> p n q", q=P)
        g_query = o_sb[:, 0:SQ]
        g_out = o_norm
        g_stat = sb("g_stat", [SQ, 4])

        xT_sb = probs[:].rearrange("p a b c -> p (a b c)")[:, 0:B * SQ]
        q_high = probs[:].rearrange("p a b c -> p (a b c)")[:, B * SQ:2 * B * SQ]
        q_low = values[:, 1].rearrange("p a b c -> p (a b c)")[:, 0:B * SQ]

        scores_ps = ctx.enter_context(nc.psum_tensor("scores_ps", [P, SCORE_SLOTS, HALF_QUADS, BANK], F32))
        o_ps = ctx.enter_context(nc.psum_tensor("o_ps", [P, BANK], F32))
        work_ps = ctx.enter_context(nc.psum_tensor("work_ps", [P, BANK], F32))

        xT_loaded = sem("xT_loaded")
        wq_loaded = sem("wq_loaded")
        wk_loaded = sem("wk_loaded")
        wv_loaded = sem("wv_loaded")
        x_loaded = sem("x_loaded")
        key_loaded = [sem("even_keys_loaded"), sem("odd_keys_loaded")]
        pads_zeroed = sem("pads_zeroed")
        consts_ready = sem("consts_ready")
        values_zeroed = sem("values_zeroed")
        ident_ready = sem("ident_ready")
        mask_step = sem("mask_step")
        q_projected = sem("q_projected")
        q_relued = sem("q_relued")
        q_split = sem("q_split")
        q_replicated = sem("q_replicated")
        q_masked = sem("q_masked")
        work_filled = sem("work_filled")
        work_free = sem("work_free")
        k_max_ready = sem("k_max_ready")
        k_high_ready = sem("k_high_ready")
        k_cent_ready = sem("k_cent_ready")
        k_low_ready = sem("k_low_ready")
        k_replicated = sem("k_replicated")
        qbd_ready = sem("qbd_ready")
        keep_ready = sem("keep_ready")
        v_ready = sem("v_ready")
        scores_ready = sem("scores_ready")
        probs_ready = sem("probs_ready")
        pv_done = sem("pv_done")
        o_copied = sem("o_copied")
        den_read = sem("den_read")
        den_inverted = sem("den_inverted")
        o_half_normed = sem("o_half_normed")
        out_ready = sem("out_ready")
        out_stored = sem("out_stored")
        bound_made = sem("bound_made")
        kept_counted = sem("kept_counted")
        selectors_ready = sem("selectors_ready")
        checks_summed = sem("checks_summed")
        check_step = sem("check_step")
        path_chosen = sem("path_chosen")
        g_loaded = sem("g_loaded")
        g_projected = sem("g_projected")
        g_values_projected = sem("g_values_projected")
        g_prepared = sem("g_prepared")
        g_keys_made = sem("g_keys_made")
        g_query_made = sem("g_query_made")
        g_scored = sem("g_scored")
        g_masked = sem("g_masked")
        g_exped = sem("g_exped")
        g_inverted = sem("g_inverted")
        g_transposed = sem("g_transposed")
        g_copied = sem("g_copied")
        g_summed = sem("g_summed")
        g_head_done = sem("g_head_done")
        g_out_made = sem("g_out_made")
        g_stored = sem("g_stored")

        WORKS = KCHUNKS + VGROUPS

        def works_before(b):
            return WORKS if isinstance(b, int) and b == 0 else (WORKS + 1) * b + WORKS - 1

        def pairs_loop(eng, first, last, body):
            with nc.Fori(0, (last - first) // 2, engines=[eng.engine], hint_back_edge=True) as i:
                for k in range(2):
                    body(first + k + 2 * i, (first + k) % 2)

        def general_path(eng, body, after=lambda: None):
            eng.wait_ge(path_chosen, 1)
            passed = eng.value_load(bounded[0:1, 0:1], min_val=0, max_val=B)
            with eng.If(passed < B):
                with nc.Fori(0, B, engines=[eng.engine]) as b:
                    body(b)
                after()

        def row(ap, b):
            return ap[b] if isinstance(b, int) else ap[bass.ds(b, 1)].rearrange("a p n -> (a p) n")

        block = ctx.enter_context(nc.Block())

        @block.sync
        def _(sp):
            def load_keys(b, parity):
                sp.dma_start(keyT[:, parity, 0:SK], row(ctxT, b)).then_inc(key_loaded[parity], 16)

            def replicate(parity, source, slots, done):
                for t in range(QUADS):
                    for s in slots:
                        sp.dma_start(k_parts[32 * s:32 * s + 32, parity, t, :].bitcast(F32),
                                     source[32 * t:32 * t + 32, :].bitcast(F32)).then_inc(done, 16)

            def spread_keys(b, parity):
                sp.wait_ge(k_high_ready, b + 1)
                replicate(parity, k_high, (0, 2), k_replicated)
                sp.wait_ge(k_low_ready, b + 1)
                replicate(parity, k_low, (1, 3), k_replicated)

            def store(b):
                sp.wait_ge(out_ready, b + 1)
                src = out_sb[:, b, :] if isinstance(b, int) else \
                    out_sb[:, bass.ds(b, 1), :].rearrange("q a d -> q (a d)")
                sp.dma_start(row(out, b), src).then_inc(out_stored, 16)

            load_keys(0, 0)
            sp.dma_start(wk_sb[:], Wk).then_inc(wk_loaded, 16)
            sp.dma_start(bk_sb[:], bk).then_inc(wk_loaded, 16)
            sp.dma_start(xT_sb.rearrange("p (b q) -> p b q", b=B), xT).then_inc(xT_loaded, 16)
            sp.dma_start(wq_sb[:], Wq).then_inc(wq_loaded, 16)
            sp.dma_start(bq_sb[:], bq).then_inc(wq_loaded, 16)
            sp.dma_start(wv_sb[:, 0:D], Wv).then_inc(wv_loaded, 16)
            sp.dma_start(bv_sb[:], bv.to_broadcast([P, D])).then_inc(wv_loaded, 16)
            load_keys(1, 1)
            sp.dma_start(x_sb[:], x.rearrange("b q d -> q b d")).then_inc(x_loaded, 16)
            spread_keys(0, 0)

            def batch(b, parity, more=True, before=True):
                if more:
                    sp.wait_ge(work_free, works_before(b))
                    load_keys(b + 2, parity)
                if before:
                    sp.wait_ge(scores_ready, UNITS * b)
                spread_keys(b + 1, 1 - parity)
                if before:
                    store(b - 1)

            batch(0, 0, before=False)
            pairs_loop(sp, 1, B - 3, batch)
            batch(B - 3, (B - 3) % 2)
            batch(B - 2, (B - 2) % 2, more=False)
            store(B - 2)
            store(B - 1)
            sp.wait_ge(out_stored, 16 * B)

            def general(b):
                sp.dma_start(keyT[:, 0, 0:SK], row(ctxT, b)).then_inc(g_loaded, 16)
                sp.wait_ge(g_out_made, b + 1)
                sp.dma_start(row(out, b), g_out[:]).then_inc(g_stored, 16)

            general_path(sp, general, lambda: sp.wait_ge(g_stored, 16 * B))

        @block.gpsimd
        def _(pool):
            nc.gpsimd.memset(keyT[:, :, SK:SKP], 0.0).then_inc(pads_zeroed, 1)
            nc.gpsimd.memset(wv_sb[:, D:VW], 1.0).then_inc(pads_zeroed, 1)
            nc.gpsimd.memset(shift_sb[:], SHIFT).then_inc(consts_ready, 1)
            nc.gpsimd.memset(values[:, 0], 0.0).then_inc(values_zeroed, 1)
            nc.gpsimd.memset(blockmask[:], 1.0).then_inc(mask_step, 1)
            pool.wait_ge(mask_step, 1)
            for s in range(SLOTS):
                part = blockmask[32 * s:32 * s + 32, :]
                nc.gpsimd.affine_select(out=part, in_=part, compare_op=ALU.is_ge, fill=0.0, base=0,
                                        pattern=[[-DH, QUAD]], channel_multiplier=1).then_inc(mask_step, 1)
            pool.wait_ge(mask_step, 1 + SLOTS)
            for s in range(SLOTS):
                part = blockmask[32 * s:32 * s + 32, :]
                nc.gpsimd.affine_select(out=part, in_=part, compare_op=ALU.is_ge, fill=0.0, base=DH - 1,
                                        pattern=[[DH, QUAD]], channel_multiplier=-1).then_inc(mask_step, 1)
            pool.wait_ge(mask_step, 1 + 2 * SLOTS)
            nc.gpsimd.memset(ident[:], 0.0).then_inc(ident_ready, 1)
            pool.wait_ge(ident_ready, 1)
            nc.gpsimd.affine_select(out=ident[:], in_=ident[:], compare_op=ALU.not_equal, fill=1.0, base=0,
                                    pattern=[[-1, P]], channel_multiplier=1).then_inc(ident_ready, 1)
            pool.wait_ge(ident_ready, 2)
            nc.gpsimd.memset(head_sum[:], 1.0).then_inc(selectors_ready, 1)
            pool.wait_ge(selectors_ready, 1)
            nc.gpsimd.affine_select(out=head_sum[:], in_=head_sum[:], compare_op=ALU.is_ge, fill=0.0, base=0,
                                    pattern=[[-DH, HEADS]], channel_multiplier=1).then_inc(selectors_ready, 1)
            pool.wait_ge(selectors_ready, 2)
            nc.gpsimd.affine_select(out=head_sum[:], in_=head_sum[:], compare_op=ALU.is_ge, fill=0.0,
                                    base=DH - 1, pattern=[[DH, HEADS]], channel_multiplier=-1
                                    ).then_inc(selectors_ready, 1)
            pool.wait_ge(selectors_ready, 3)
            nc.gpsimd.memset(ones[:], 1.0).then_inc(selectors_ready, 1)
            pool.wait_ge(q_replicated, 16 * REPLICAS)
            nc.gpsimd.memset(values[:, 1], 0.0).then_inc(values_zeroed, 1)

        @block.scalar
        def _(act):
            for part, source, slots in ((1, q_high, (0, 1)), (2, q_low, (2, 3))):
                act.wait_ge(q_split, part)
                for t in range(QUADS):
                    for s in slots:
                        act.dma_start(query_rep[32 * s:32 * s + 32, t, :].bitcast(F32),
                                      source[32 * t:32 * t + 32, :]).then_inc(q_replicated, 16)
            act.wait_ge(consts_ready, 1)
            act.wait_ge(q_replicated, 16 * REPLICAS)

            def batch(b, parity):
                for u in range(UNITS):
                    act.wait_ge(scores_ready, UNITS * b + u + 1)
                    if not isinstance(b, int) or b > 0 or u >= PROB_SLOTS:
                        act.wait_ge(pv_done, UNITS * b + u + 1 - PROB_SLOTS)
                    nc.scalar.activation(probs[:, u % PROB_SLOTS], scores_ps[:, u % SCORE_SLOTS, :, 0:QCOLS],
                                         ACT.Exp, bias=shift_sb[:], scale=SCALE).then_inc(probs_ready, 1)

            batch(0, 0)
            pairs_loop(act, 1, B - 1, batch)
            batch(B - 1, 1)

            def general(b):
                with nc.Fori(0, HEADS, engines=[act.engine]) as h:
                    n = b * HEADS + h
                    act.wait_ge(g_masked, 4 * n + 4)
                    nc.scalar.activation(g_scores[:, 0:SK], g_scores[:, 0:SK], ACT.Exp, bias=g_stat[:, 1:2],
                                         accum_out=g_stat[:, 2:3]).then_inc(g_exped, 1)

            general_path(act, general)

        @block.tensor
        def _(pe):
            def work(index):
                if not isinstance(index, int) or index > 0:
                    pe.wait_ge(work_free, index)

            def project_keys(parity, c):
                return nc.tensor.matmul(work_ps[:], wk_sb[:], keyT[:, parity, c * BANK:(c + 1) * BANK],
                                        start=True, stop=True)

            def project_values(parity, g):
                for n in range(VGROUP):
                    kt = g * VGROUP + n
                    mm = nc.tensor.matmul(work_ps[:, n * VW:(n + 1) * VW], keyT[:, parity, kt * P:(kt + 1) * P],
                                          wv_sb[:], start=True, stop=True)
                return mm

            def transpose_outputs():
                for n in range(HALVES * PAIR):
                    mm = nc.tensor.transpose(work_ps[0:SQ, n * P:(n + 1) * P], o_sb[:, n * SQ:(n + 1) * SQ],
                                             ident[:])
                return mm

            def prepare(b, parity, k, index):
                if k == 0:
                    pe.wait_ge(key_loaded[parity], 8 * (b - parity) + 16)
                work(index)
                if k < KCHUNKS:
                    project_keys(parity, k).then_inc(work_filled, 1)
                else:
                    project_values(parity, k - KCHUNKS).then_inc(work_filled, 1)

            def scores(b, parity, u):
                kt, half = divmod(u, HALVES)
                if u == 0:
                    pe.wait_ge(k_replicated, 16 * REPLICAS * (b + 1))
                    pe.wait_ge(qbd_ready, b + 1)
                if not isinstance(b, int) or b > 0 or u >= SCORE_SLOTS:
                    pe.wait_ge(probs_ready, UNITS * b + u + 1 - SCORE_SLOTS)
                for n in range(HALF_QUADS):
                    t = half * HALF_QUADS + n
                    mm = nc.tensor.matmul(scores_ps[:, u % SCORE_SLOTS, n, 0:QCOLS],
                                          k_parts[:, parity, t, kt * P:(kt + 1) * P],
                                          query_bd[:, parity, t, :], start=True, stop=True)
                mm.then_inc(scores_ready, 1)

            def value_products(b, parity, u):
                kt, half = divmod(u, HALVES)
                if u == 0:
                    pe.wait_ge(v_ready, (KT + 1) * (b + 1))
                    if not isinstance(b, int) or b > 0:
                        pe.wait_ge(o_copied, b)
                pe.wait_ge(probs_ready, UNITS * b + u + 1)
                for c in range(HALF_PAIRS):
                    n, off = divmod(c * PCOLS, QCOLS)
                    mm = nc.tensor.matmul(
                        o_ps[c * VCOLS:(c + 1) * VCOLS, half * PCOLS:(half + 1) * PCOLS],
                        values[:, parity, kt, half * HALF_PAIRS + c, :],
                        probs[:, u % PROB_SLOTS, n, off:off + PCOLS],
                        start=(u == 0), stop=(kt == KT - 1), skip_group_check=True)
                mm.then_inc(pv_done, 1)

            OUT_STEP = 4
            PREPARE = {0: 0, 1: 1, 2: 2, 8: 3, 11: 4, 14: 5, 17: 6}

            def batch(b, parity, first=False, last=False):
                used = works_before(b)
                for u in range(UNITS):
                    if u + LEAD < UNITS:
                        scores(b, parity, u + LEAD)
                    elif not last:
                        scores(b + 1, 1 - parity, u + LEAD - UNITS)
                    if not last and u in PREPARE:
                        prepare(b + 1, 1 - parity, PREPARE[u], used)
                        used = used + 1
                    if not first and u == OUT_STEP:
                        work(used)
                        pe.wait_ge(o_copied, b)
                        transpose_outputs().then_inc(work_filled, 1)
                        used = used + 1
                    value_products(b, parity, u)
                return used

            pe.wait_ge(wk_loaded, 32)
            pe.wait_ge(pads_zeroed, 2)
            for k in range(KCHUNKS):
                prepare(0, 0, k, k)
            pe.wait_ge(xT_loaded, 16)
            pe.wait_ge(wq_loaded, 32)
            for g in range(B // QB):
                nc.tensor.matmul(scores_ps[:].rearrange("p a b c -> p (a b) c")[:, g, 0:QB * SQ], wq_sb[:],
                                 xT_sb[:, g * QB * SQ:(g + 1) * QB * SQ], start=True, stop=True
                                 ).then_inc(q_projected, 1)
            pe.wait_ge(wv_loaded, 32)
            for k in range(KCHUNKS, WORKS):
                prepare(0, 0, k, k)
            pe.wait_ge(q_relued, B // QB)
            pe.wait_ge(ident_ready, 2)
            for u in range(LEAD):
                scores(0, 0, u)
            batch(0, 0, first=True)
            pairs_loop(pe, 1, B - 1, batch)
            used = batch(B - 1, 1, last=True)
            work(used)
            pe.wait_ge(o_copied, B)
            transpose_outputs().then_inc(work_filled, 1)

            pe.wait_ge(selectors_ready, 4)
            pe.wait_ge(work_free, used + 1)
            pe.wait_ge(bound_made, B)
            nc.tensor.matmul(work_ps[0:B, 0:HEADS], bound_terms[:], head_sum[:], start=True, stop=True)
            pe.wait_ge(kept_counted, B)
            nc.tensor.matmul(work_ps[0:B, HEADS:HEADS + 1], kept_keys[:], ones[:, 0:1], start=True, stop=True
                             ).then_inc(checks_summed, 1)
            pe.wait_ge(check_step, 4)
            nc.tensor.matmul(work_ps[0:1, 0:1], batch_checks[:, 3:4], ones[0:B, 0:1], start=True, stop=True
                             ).then_inc(checks_summed, 1)

            banks = scores_ps[:].rearrange("p a b c -> p (a b) c")

            def general(b):
                pe.wait_ge(g_loaded, 16 * (b + 1))
                for c in range(KCHUNKS):
                    nc.tensor.matmul(banks[:, c, :], wk_sb[:], keyT[:, 0, c * BANK:(c + 1) * BANK],
                                     start=True, stop=True)
                    nc.tensor.matmul(banks[:, KCHUNKS + c, :], ones[:], keyT[:, 0, c * BANK:(c + 1) * BANK],
                                     start=True, stop=True).then_inc(g_projected, 1)
                pe.wait_ge(g_keys_made, 3 * (b + 1))
                for kt in range(KT):
                    c, n = divmod(kt, BANK // P)
                    nc.tensor.matmul(banks[:, c, n * P:(n + 1) * P], keyT[:, 0, kt * P:(kt + 1) * P],
                                     wv_sb[:, 0:D], start=True, stop=True).then_inc(g_values_projected, 1)
                with nc.Fori(0, HEADS, engines=[pe.engine]) as h:
                    n = b * HEADS + h
                    pe.wait_ge(g_prepared, 2 * (b + 1))
                    pe.wait_ge(g_query_made, n + 1)
                    for c in range(KCHUNKS):
                        mm = nc.tensor.matmul(banks[0:SQ, c, :], g_query, g_keys[:, c * BANK:(c + 1) * BANK],
                                              start=True, stop=True)
                    mm.then_inc(g_scored, 1)
                    pe.wait_ge(g_exped, n + 1)
                    for kt in range(KT):
                        c, m = divmod(kt, BANK // P)
                        mm = nc.tensor.transpose(banks[:, KCHUNKS + c, m * P:m * P + SQ],
                                                 g_scores[:, kt * P:(kt + 1) * P], ident[0:SQ, 0:SQ])
                    mm.then_inc(g_transposed, 1)
                    pe.wait_ge(g_copied, n + 1)
                    for kt in range(KT):
                        mm = nc.tensor.matmul(work_ps[0:SQ, 0:DH], g_probsT[:, kt, 0:SQ],
                                              g_values[:, kt, bass.ds(h * DH, DH)],
                                              start=(kt == 0), stop=(kt == KT - 1))
                    mm.then_inc(g_summed, 1)

            general_path(pe, general)

        @block.vector
        def _(dve):
            v = nc.vector

            def center_keys(b, k0, before):
                for c in range(KCHUNKS):
                    dve.wait_ge(work_filled, k0 + c + 1)
                    if c == 0 and before:
                        dve.wait_ge(k_low_ready, b)
                    v.tensor_scalar(k_raw[:, c * BANK:(c + 1) * BANK], work_ps[:], bk_sb[:], None, ALU.add
                                    ).then_inc(work_free, 1)
                dve.wait_ge(work_free, k0 + KCHUNKS)
                v.tensor_reduce(k_chunk_max[:, 0:1], k_raw[:], AX.X, ALU.max).then_inc(k_max_ready, 1)
                dve.wait_ge(k_max_ready, 2 * b + 1)
                v.tensor_scalar(k_max[:, 0:1], k_chunk_max[:, 0:1], 0.0, None, ALU.max).then_inc(k_max_ready, 1)
                dve.wait_ge(k_max_ready, 2 * b + 2)
                if before:
                    dve.wait_ge(k_replicated, 16 * REPLICAS * b)
                v.tensor_scalar(k_high[:], k_raw[:], 0.0, k_max[:, 0:1], ALU.max, ALU.subtract
                                ).then_inc(k_high_ready, 1)
                v.tensor_scalar(k_cent[:], k_raw[:], 0.0, k_max[:, 0:1], ALU.max, ALU.subtract
                                ).then_inc(k_cent_ready, 1)
                dve.wait_ge(k_high_ready, b + 1)
                dve.wait_ge(k_cent_ready, b + 1)
                v.tensor_tensor(k_low[:], k_cent[:], k_high[:].bitcast(F32), ALU.subtract
                                ).then_inc(k_low_ready, 1)

            def bound_scores(b):
                at = slice(b, b + 1) if isinstance(b, int) else bass.ds(b, 1)
                v.tensor_tensor(bound_terms[:, at], k_max[:, 0:1], q_max[:, at], ALU.mult
                                ).then_inc(bound_made, 1)

            def finish_values(b, parity, g, index, before):
                rows = slice(g * VGROUP, (g + 1) * VGROUP)
                dve.wait_ge(work_filled, index + 1)
                work = work_ps[:, 0:VGROUP * VW].rearrange("p (n w) -> p n w", w=VW)
                v.tensor_scalar(keep[:, rows], work[:, :, D], 0.0, None, ALU.not_equal).then_inc(keep_ready, 1)
                v.tensor_tensor(v_biased[:, g % 2], work[:, :, 0:D],
                                bv_sb[:].unsqueeze(1).to_broadcast([P, VGROUP, D]), ALU.add
                                ).then_inc(work_free, 1)
                dve.wait_ge(keep_ready, VGROUPS * b + g + 1)
                dve.wait_ge(work_free, index + 1)
                for n in range(VGROUP):
                    kt = g * VGROUP + n
                    v.tensor_scalar(values[:, parity, kt, :, 0:PAIR * DH],
                                    v_biased[:, g % 2, n].rearrange("p (a w) -> p a w", w=PAIR * DH),
                                    0.0, keep[:, kt:kt + 1], ALU.max, ALU.mult).then_inc(v_ready, 1)

            def finish_keep(b, parity):
                v.tensor_copy(values[:, parity, :, :, PAIR * DH],
                              keep[:].unsqueeze(2).to_broadcast([P, KT, PAIRS])).then_inc(v_ready, 1)
                at = slice(b, b + 1) if isinstance(b, int) else bass.ds(b, 1)
                v.tensor_reduce(kept_keys[:, at], keep[:], AX.X, ALU.add).then_inc(kept_counted, 1)

            def spread_queries(b, parity):
                src = query_rep[:, :, b * SQ:(b + 1) * SQ] if isinstance(b, int) else \
                    query_rep[:, :, bass.ds(b * SQ, SQ)]
                for t in range(QUADS):
                    ins = v.tensor_tensor(
                        query_bd[:, parity, t, :].rearrange("p (h q) -> p h q", h=QUAD),
                        src[:, t].bitcast(F32).unsqueeze(1).to_broadcast([P, QUAD, SQ]),
                        blockmask[:].unsqueeze(2).to_broadcast([P, QUAD, SQ]), ALU.mult)
                ins.then_inc(qbd_ready, 1)

            def copy_outputs(b):
                dve.wait_ge(pv_done, UNITS * (b + 1))
                v.tensor_copy(o_sb[:], o_ps[:, 0:HALVES * PCOLS]).then_inc(o_copied, 1)

            def finish_outputs(b, index):
                dve.wait_ge(work_filled, index + 1)
                t = work_ps[0:SQ, :].rearrange("q (rj c w) -> q rj c w", c=HALF_PAIRS, w=VCOLS)
                v.tensor_scalar(inv_den[:], t[:, :, :, PAIR * DH], DEN_FLOOR, None, ALU.max).then_inc(den_read, 1)
                dve.wait_ge(den_read, b + 1)
                v.reciprocal(inv_den[:], inv_den[:]).then_inc(den_inverted, 1)
                dve.wait_ge(den_inverted, b + 1)
                o = o_norm[:].rearrange("q (r c j d) -> q r c j d", r=HALVES, c=HALF_PAIRS, j=PAIR)
                t = work_ps[0:SQ, :].rearrange("q (r j c w) -> q r j c w", r=HALVES, j=PAIR, w=VCOLS)
                i = inv_den[:].rearrange("q (r j) c -> q r j c", j=PAIR)
                for j, done in ((0, o_half_normed), (1, work_free)):
                    v.tensor_tensor(o[:, :, :, j, :], t[:, :, j, :, j * DH:(j + 1) * DH],
                                    i[:, :, j, :].unsqueeze(3).to_broadcast([SQ, HALVES, HALF_PAIRS, DH]),
                                    ALU.mult).then_inc(done, 1)
                dve.wait_ge(o_half_normed, b + 1)
                dve.wait_ge(work_free, index + 1)
                at = slice(b, b + 1) if isinstance(b, int) else bass.ds(b, 1)
                v.scalar_tensor_tensor(out=out_sb[:, at, :].rearrange("q a d -> q (a d)"), in0=o_norm[:],
                                       scalar=q_mask[:, at], in1=x_sb[:, at, :].rearrange("q a d -> q (a d)"),
                                       op0=ALU.mult, op1=ALU.add).then_inc(out_ready, 1)

            def batch(b, parity, first=False, last=False):
                used = works_before(b)
                if not first:
                    copy_outputs(b - 1)
                if not last:
                    center_keys(b + 1, used, True)
                    used = used + KCHUNKS
                    bound_scores(b + 1)
                if not first:
                    finish_outputs(b - 1, used)
                    used = used + 1
                if not last:
                    for g in range(VGROUPS):
                        finish_values(b + 1, 1 - parity, g, used, True)
                        used = used + 1
                    finish_keep(b + 1, 1 - parity)
                    spread_queries(b + 1, 1 - parity)
                return used

            dve.wait_ge(wk_loaded, 32)
            center_keys(0, 0, False)
            dve.wait_ge(wq_loaded, 32)
            for g in range(B // QB):
                dve.wait_ge(q_projected, g + 1)
                v.tensor_scalar(queryT[:, g * QB * SQ:(g + 1) * QB * SQ],
                                scores_ps[:].rearrange("p a b c -> p (a b) c")[:, g, 0:QB * SQ],
                                bq_sb[:], 0.0, ALU.add, ALU.max).then_inc(q_relued, 1)
            dve.wait_ge(q_relued, B // QB)
            v.tensor_copy(q_high.bitcast(F32R), queryT[:]).then_inc(q_split, 1)
            dve.wait_ge(q_split, 1)
            v.tensor_tensor(q_low.bitcast(F32R), queryT[:], q_high, ALU.subtract).then_inc(q_split, 1)
            dve.wait_ge(wv_loaded, 32)
            dve.wait_ge(values_zeroed, 1)
            for g in range(VGROUPS):
                finish_values(0, 0, g, KCHUNKS + g, False)
            finish_keep(0, 0)
            dve.wait_ge(mask_step, 1 + 2 * SLOTS)
            dve.wait_ge(q_replicated, 16 * REPLICAS)
            spread_queries(0, 0)
            dve.wait_ge(x_loaded, 16)
            v.tensor_reduce(q_sum[:], x_sb[:], AX.X, ALU.add).then_inc(q_masked, 1)
            dve.wait_ge(q_masked, 1)
            v.tensor_scalar(q_mask[:], q_sum[:], 0.0, None, ALU.not_equal).then_inc(q_masked, 1)
            v.tensor_reduce(q_max[:], queryT[:].rearrange("p (b q) -> p b q", b=B), AX.X, ALU.max
                            ).then_inc(q_masked, 1)
            dve.wait_ge(q_masked, 3)
            bound_scores(0)
            dve.wait_ge(values_zeroed, 2)
            batch(0, 0, first=True)
            pairs_loop(dve, 1, B - 1, batch)
            used = batch(B - 1, 1, last=True)
            copy_outputs(B - 1)
            finish_outputs(B - 1, used)

            dve.wait_ge(checks_summed, 1)
            v.tensor_reduce(batch_checks[:, 0:1], work_ps[0:B, 0:HEADS], AX.X, ALU.max).then_inc(check_step, 1)
            v.tensor_scalar(batch_checks[:, 2:3], work_ps[0:B, HEADS:HEADS + 1], 0.5, None, ALU.is_ge
                            ).then_inc(check_step, 1)
            dve.wait_ge(check_step, 2)
            v.tensor_scalar(batch_checks[:, 1:2], batch_checks[:, 0:1], BOUND_LIMIT / SCALE, None, ALU.is_le
                            ).then_inc(check_step, 1)
            dve.wait_ge(check_step, 3)
            v.tensor_tensor(batch_checks[:, 3:4], batch_checks[:, 1:2], batch_checks[:, 2:3], ALU.mult
                            ).then_inc(check_step, 1)
            dve.wait_ge(checks_summed, 2)
            v.tensor_copy(bounded[:], work_ps[0:1, 0:1]).then_inc(path_chosen, 1)

            banks = scores_ps[:].rearrange("p a b c -> p (a b) c")

            def flat(ap, parts=P):
                return ap.rearrange("p (c n) -> p c n", n=BANK)

            def general(b):
                at = bass.ds(b, 1)
                dve.wait_ge(g_projected, KCHUNKS * (b + 1))
                v.tensor_scalar(flat(g_keys[:]), banks[:, 0:KCHUNKS, :], bk_sb[:], 0.0, ALU.add, ALU.max
                                ).then_inc(g_keys_made, 1)
                v.tensor_scalar(flat(g_keep[:]), banks[:, KCHUNKS:2 * KCHUNKS, :], 0.0, None, ALU.not_equal
                                ).then_inc(g_keys_made, 1)
                dve.wait_ge(g_keys_made, 3 * b + 2)
                v.tensor_scalar(g_mask, g_keep[:], -1.0, NEG, ALU.add, ALU.mult).then_inc(g_keys_made, 1)
                dve.wait_ge(g_values_projected, KT * (b + 1))
                for c in range(KCHUNKS):
                    n = BANK // P
                    ins = v.tensor_tensor(g_values[:, c * n:(c + 1) * n, :],
                                          banks[:, c, :].rearrange("p (n w) -> p n w", w=D),
                                          bv_sb[:].unsqueeze(1).to_broadcast([P, n, D]), ALU.add)
                ins.then_inc(g_prepared, 1)
                dve.wait_ge(g_prepared, 2 * b + 1)
                v.tensor_scalar(g_values, g_values, 0.0, None, ALU.max).then_inc(g_prepared, 1)
                with nc.Fori(0, HEADS, engines=[dve.engine]) as h:
                    n = b * HEADS + h
                    dve.wait_ge(g_keys_made, 3 * (b + 1))
                    v.tensor_scalar(g_query, queryT[:, bass.ds(b * SQ, SQ)], head_sum[:, bass.ds(h, 1)], None,
                                    ALU.mult).then_inc(g_query_made, 1)
                    dve.wait_ge(g_scored, n + 1)
                    v.scalar_tensor_tensor(out=flat(g_scores, SQ), in0=banks[0:SQ, 0:KCHUNKS, :], scalar=SCALE,
                                           in1=flat(g_keep[0:SQ, :]), op0=ALU.mult, op1=ALU.mult
                                           ).then_inc(g_masked, 1)
                    dve.wait_ge(g_masked, 4 * n + 1)
                    v.tensor_tensor(g_scores, g_scores, g_mask[0:SQ], ALU.add).then_inc(g_masked, 1)
                    dve.wait_ge(g_masked, 4 * n + 2)
                    v.tensor_reduce(g_stat[:, 0:1], g_scores[:, 0:SK], AX.X, ALU.max).then_inc(g_masked, 1)
                    dve.wait_ge(g_masked, 4 * n + 3)
                    v.memset(g_scores[:, SK:SKP], 0.0)
                    v.tensor_scalar(g_stat[:, 1:2], g_stat[:, 0:1], -1.0, None, ALU.mult).then_inc(g_masked, 1)
                    dve.wait_ge(g_exped, n + 1)
                    v.reciprocal(g_stat[:, 3:4], g_stat[:, 2:3]).then_inc(g_inverted, 1)
                    dve.wait_ge(g_transposed, n + 1)
                    for c in range(KCHUNKS):
                        m = BANK // P
                        ins = v.tensor_copy(g_probsT[:, c * m:(c + 1) * m, 0:SQ],
                                            banks[:, KCHUNKS + c, :].rearrange("p (n q) -> p n q", q=P)[:, :, 0:SQ])
                    ins.then_inc(g_copied, 1)
                    dve.wait_ge(g_summed, n + 1)
                    dve.wait_ge(g_inverted, n + 1)
                    v.tensor_scalar(g_out[:, bass.ds(h * DH, DH)], work_ps[0:SQ, 0:DH], g_stat[:, 3:4], None,
                                    ALU.mult).then_inc(g_head_done, 1)
                dve.wait_ge(g_head_done, HEADS * (b + 1))
                v.scalar_tensor_tensor(out=g_out[:], in0=g_out[:], scalar=q_mask[:, at],
                                       in1=x_sb[:, at, :].rearrange("q a d -> q (a d)"),
                                       op0=ALU.mult, op1=ALU.add).then_inc(g_out_made, 1)
                dve.wait_ge(g_stored, 16 * (b + 1))

            general_path(dve, general)


def kernel(**inputs):
    import numpy as np
    import concourse.bacc as bacc
    from concourse.bass_utils import run_bass_kernel_spmd

    a = {name: np.asarray(value) for name, value in inputs.items()}
    arrays = {
        "x": a["x"],
        "xT": np.ascontiguousarray(a["x"].transpose(2, 0, 1)),
        "ctxT": np.ascontiguousarray(a["ctx_1024"].transpose(0, 2, 1)),
        "Wq": a["L0_xattn_Wq"],
        "bq": a["L0_xattn_bq"].reshape(-1, 1),
        "Wk": a["L0_xattn_Wk"],
        "bk": a["L0_xattn_bk"].reshape(-1, 1),
        "Wv": a["L0_xattn_Wv"],
        "bv": a["L0_xattn_bv"].reshape(1, -1),
    }
    nc = bacc.Bacc("TRN2", target_bir_lowering=False, num_devices=1)
    args = [nc.dram_tensor(f"in_{name}", value.shape, mybir.dt.from_np(value.dtype), kind="ExternalInput").ap()
            for name, value in arrays.items()]
    args.append(nc.dram_tensor("out", a["x"].shape, F32, kind="ExternalOutput").ap())
    attention(nc, *args)
    r = run_bass_kernel_spmd(nc, [{f"in_{name}": value for name, value in arrays.items()}], core_ids=[0])
    return r.results[0]["out"]
```

```python
from contextlib import ExitStack

import concourse.bass as bass
from concourse import mybir

F32 = mybir.dt.float32
F32R = mybir.dt.float32r
I32 = mybir.dt.int32
ALU = mybir.AluOpType
ACT = mybir.ActivationFunctionType
AX = mybir.AxisListType

P = 128
BANK = 512

SLOTS = 4
HEADS = 16
QUAD = 4
PAIR = 2
VCOLS = 32
SCORE_SLOTS = 3
PROB_SLOTS = 4
LEAD = 2
SHIFT = 40.0
BOUND_LIMIT = 100.0
DEN_FLOOR = 1e-30
NEG = float(2 ** 32)


def attention(
    nc: bass.Bass,
    x: bass.AP,
    xT: bass.AP,
    ctxT: bass.AP,
    Wq: bass.AP,
    bq: bass.AP,
    Wk: bass.AP,
    bk: bass.AP,
    Wv: bass.AP,
    bv: bass.AP,
    out: bass.AP,
):
    B, SQ, D = x.shape
    SK = ctxT.shape[2]
    DH = D // HEADS
    SCALE = 1.0 / DH ** 0.5
    KT = -(-SK // P)
    SKP = KT * P
    QUADS = HEADS // QUAD
    PAIRS = HEADS // PAIR
    HALVES = 2
    HALF_PAIRS = PAIRS // HALVES
    HALF_QUADS = QUADS // HALVES
    UNITS = KT * HALVES
    QCOLS = QUAD * SQ
    PCOLS = PAIR * SQ
    VW = D + 1
    VGROUP = 3
    VGROUPS = KT // VGROUP
    KCHUNKS = SKP // BANK
    QB = 4
    QGROUPS = B // QB
    assert D == P and DH * QUAD == 32 and VGROUP * VW <= BANK and HALF_PAIRS * VCOLS == P
    assert UNITS % SCORE_SLOTS == 0 and UNITS % PROB_SLOTS == 0 and B % 2 == 0 and B % QB == 0
    assert QB * SQ <= BANK and 2 * QB * SQ <= SK and QGROUPS <= QUADS and QCOLS <= BANK and HALVES * PCOLS <= BANK
    KPIECES = 2
    Q_BANKS = (0, 3, 4, 5)
    K_BANKS = (1, 2, 0)
    V_BANKS = (1, 2, 3, 4)
    REPLICAS = SLOTS * QUADS

    ctx = ExitStack()
    with ctx:
        def sb(name, shape, dt=F32):
            return ctx.enter_context(nc.sbuf_tensor(name, shape, dt))

        def sem(name):
            return ctx.enter_context(nc.semaphore(name))

        wq_sb = sb("wq_sb", [P, D])
        wk_sb = sb("wk_sb", [P, D])
        wv_sb = sb("wv_sb", [P, VW])
        bq_sb = sb("bq_sb", [P, 1])
        bk_sb = sb("bk_sb", [P, 1])
        bv_sb = sb("bv_sb", [P, D])
        ident = sb("ident", [P, P])
        blockmask = sb("blockmask", [P, QUAD])
        shift_sb = sb("shift_sb", [P, 1])
        keyT = sb("keyT", [P, 2, SKP])
        queryT = sb("queryT", [P, B * SQ])
        query_rep = sb("query_rep", [P, QUADS, B * SQ], F32R)
        query_bd = sb("query_bd", [P, 2, QUADS, QCOLS], F32R)
        k_raw = sb("k_raw", [P, SKP])
        k_cent = sb("k_cent", [P, SKP])
        k_high = sb("k_high", [P, SK], F32R)
        k_low = sb("k_low", [P, SK], F32R)
        k_parts = sb("k_parts", [P, 2, QUADS, SKP], F32R)
        k_chunk_max = sb("k_chunk_max", [P, KCHUNKS])
        k_max = sb("k_max", [P, 2])
        v_biased = sb("v_biased", [P, 2, VGROUP, D])
        keep = sb("keep", [P, KT])
        values = sb("values", [P, 2, KT, PAIRS, VCOLS])
        probs = sb("probs", [P, PROB_SLOTS, HALF_QUADS, QCOLS])
        o_sb = sb("o_sb", [P, HALVES * PCOLS])
        inv_den = sb("inv_den", [SQ, HALVES * PAIR, HALF_PAIRS])
        o_norm = sb("o_norm", [SQ, D])
        x_sb = sb("x_sb", [SQ, B, D])
        q_sum = sb("q_sum", [SQ, B])
        q_mask = sb("q_mask", [SQ, B])
        out_sb = sb("out_sb", [SQ, B, D])
        q_max = sb("q_max", [P, B])

        head_sum = sb("head_sum", [P, HEADS])
        ones = sb("ones", [P, P])
        bound_terms = sb("bound_terms", [P, B])
        kept_keys = sb("kept_keys", [P, B])
        batch_checks = sb("batch_checks", [B, 4])
        bounded = sb("bounded", [1, 1], I32)

        g_keys = k_raw
        g_keep = k_cent
        g_values = values[:, 0].rearrange("p a b c -> p (a b c)")[:, 0:KT * D].rearrange("p (n w) -> p n w", w=D)
        g_mask = probs[:].rearrange("p a b c -> p (a b c)")[:, 0:SKP]
        g_scores = probs[:].rearrange("p a b c -> p (a b c)")[0:SQ, SKP:2 * SKP]
        g_probsT = values[:, 1].rearrange("p a b c -> p (a b c)")[:, 0:KT * P].rearrange("p (n q) -> p n q", q=P)
        g_query = o_sb[:, 0:SQ]
        g_out = o_norm
        g_stat = sb("g_stat", [SQ, 4])

        xT_sb = values[:, 1].rearrange("p a b c -> p (a b c)")[:, 0:B * SQ]
        q_high = k_parts[:, 1, 0:QGROUPS, 0:QB * SQ]
        q_low = k_parts[:, 1, 0:QGROUPS, QB * SQ:2 * QB * SQ]

        scores_ps = ctx.enter_context(nc.psum_tensor("scores_ps", [P, SCORE_SLOTS, HALF_QUADS, BANK], F32))
        o_ps = ctx.enter_context(nc.psum_tensor("o_ps", [P, BANK], F32))
        work_ps = ctx.enter_context(nc.psum_tensor("work_ps", [P, BANK], F32))

        first_xT_loaded = sem("first_xT_loaded")
        xT_loaded = sem("xT_loaded")
        wq_loaded = sem("wq_loaded")
        wk_loaded = sem("wk_loaded")
        wv_loaded = sem("wv_loaded")
        x_loaded = sem("x_loaded")
        first_keys_loaded = [sem(f"first_keys_loaded{c}") for c in range(KCHUNKS)]
        key_loaded = [sem("even_keys_loaded"), sem("odd_keys_loaded")]
        pads_zeroed = sem("pads_zeroed")
        consts_ready = sem("consts_ready")
        values_zeroed = sem("values_zeroed")
        ident_ready = sem("ident_ready")
        mask_step = sem("mask_step")
        q_projected = sem("q_projected")
        q_relued = sem("q_relued")
        q_split = sem("q_split")
        first_q_replicated = sem("first_q_replicated")
        q_replicated = sem("q_replicated")
        q_masked = sem("q_masked")
        first_projected = sem("first_projected")
        first_evacuated = sem("first_evacuated")
        work_filled = sem("work_filled")
        work_free = sem("work_free")
        k_max_ready = sem("k_max_ready")
        k_high_ready = sem("k_high_ready")
        k_cent_ready = sem("k_cent_ready")
        k_low_ready = sem("k_low_ready")
        k_replicated = sem("k_replicated")
        qbd_ready = sem("qbd_ready")
        keep_ready = sem("keep_ready")
        v_ready = sem("v_ready")
        scores_ready = sem("scores_ready")
        probs_ready = sem("probs_ready")
        pv_done = sem("pv_done")
        o_copied = sem("o_copied")
        den_read = sem("den_read")
        den_inverted = sem("den_inverted")
        o_half_normed = sem("o_half_normed")
        out_ready = sem("out_ready")
        out_stored = sem("out_stored")
        bound_made = sem("bound_made")
        kept_counted = sem("kept_counted")
        selectors_ready = sem("selectors_ready")
        checks_summed = sem("checks_summed")
        check_step = sem("check_step")
        path_chosen = sem("path_chosen")
        g_loaded = sem("g_loaded")
        g_projected = sem("g_projected")
        g_values_projected = sem("g_values_projected")
        g_prepared = sem("g_prepared")
        g_keys_made = sem("g_keys_made")
        g_query_made = sem("g_query_made")
        g_scored = sem("g_scored")
        g_masked = sem("g_masked")
        g_exped = sem("g_exped")
        g_inverted = sem("g_inverted")
        g_transposed = sem("g_transposed")
        g_copied = sem("g_copied")
        g_summed = sem("g_summed")
        g_head_done = sem("g_head_done")
        g_out_made = sem("g_out_made")
        g_stored = sem("g_stored")

        WORKS = KCHUNKS + VGROUPS

        def works_before(b):
            return 0 if isinstance(b, int) and b == 0 else (WORKS + 1) * b - 1

        def pairs_loop(eng, first, last, body):
            with nc.Fori(0, (last - first) // 2, engines=[eng.engine], hint_back_edge=True) as i:
                for k in range(2):
                    body(first + k + 2 * i, (first + k) % 2)

        def general_path(eng, body, after=lambda: None):
            eng.wait_ge(path_chosen, 1)
            passed = eng.value_load(bounded[0:1, 0:1], min_val=0, max_val=B)
            with eng.If(passed < B):
                with nc.Fori(0, B, engines=[eng.engine]) as b:
                    body(b)
                after()

        def row(ap, b):
            return ap[b] if isinstance(b, int) else ap[bass.ds(b, 1)].rearrange("a p n -> (a p) n")

        block = ctx.enter_context(nc.Block())

        @block.sync
        def _(sp):
            def load_keys(b, parity):
                sp.dma_start(keyT[:, parity, 0:SK], row(ctxT, b)).then_inc(key_loaded[parity], 16)

            def replicate(parity, source, slots):
                for t in range(QUADS):
                    for s in slots:
                        sp.dma_start(k_parts[32 * s:32 * s + 32, parity, t, 0:SK].bitcast(F32),
                                     source[32 * t:32 * t + 32, :].bitcast(F32)).then_inc(k_replicated, 16)

            def spread_keys(b, parity):
                sp.wait_ge(k_high_ready, b + 1)
                replicate(parity, k_high, (0, 2))
                sp.wait_ge(k_low_ready, b + 1)
                replicate(parity, k_low, (1, 3))

            def store(b):
                sp.wait_ge(out_ready, b + 1)
                src = out_sb[:, b, :] if isinstance(b, int) else \
                    out_sb[:, bass.ds(b, 1), :].rearrange("q a d -> q (a d)")
                sp.dma_start(row(out, b), src).then_inc(out_stored, 16)

            sp.dma_start(wk_sb[:], Wk).then_inc(wk_loaded, 16)
            sp.dma_start(bk_sb[:], bk).then_inc(wk_loaded, 16)
            for c in range(KCHUNKS):
                end = min((c + 1) * BANK, SK)
                sp.dma_start(keyT[:, 0, c * BANK:end], ctxT[0][:, c * BANK:end]
                             ).then_inc(first_keys_loaded[c], 16)
            sp.dma_start(wv_sb[:, 0:D], Wv).then_inc(wv_loaded, 16)
            sp.dma_start(bv_sb[:], bv.to_broadcast([P, D])).then_inc(wv_loaded, 16)
            sp.dma_start(xT_sb[:, QB * SQ:].rearrange("p (b q) -> p b q", q=SQ), xT[:, QB:, :]
                         ).then_inc(xT_loaded, 16)
            sp.dma_start(x_sb[:], x.rearrange("b q d -> q b d")).then_inc(x_loaded, 16)
            load_keys(1, 1)
            spread_keys(0, 0)

            def batch(b, parity, more=True, before=True):
                if more:
                    if before:
                        sp.wait_ge(work_free, works_before(b))
                    else:
                        sp.wait_ge(first_evacuated, KCHUNKS + VGROUPS)
                    load_keys(b + 2, parity)
                if before:
                    sp.wait_ge(scores_ready, UNITS * b)
                else:
                    sp.wait_ge(first_q_replicated, 16 * REPLICAS)
                    sp.wait_ge(q_replicated, 16 * REPLICAS)
                spread_keys(b + 1, 1 - parity)
                if before:
                    store(b - 1)

            batch(0, 0, before=False)
            pairs_loop(sp, 1, B - 3, batch)
            batch(B - 3, (B - 3) % 2)
            batch(B - 2, (B - 2) % 2, more=False)
            store(B - 2)
            store(B - 1)
            sp.wait_ge(out_stored, 16 * B)

            def general(b):
                sp.dma_start(keyT[:, 0, 0:SK], row(ctxT, b)).then_inc(g_loaded, 16)
                sp.wait_ge(g_out_made, b + 1)
                sp.dma_start(row(out, b), g_out[:]).then_inc(g_stored, 16)

            general_path(sp, general, lambda: sp.wait_ge(g_stored, 16 * B))

        @block.gpsimd
        def _(pool):
            nc.gpsimd.memset(keyT[:, :, SK:SKP], 0.0).then_inc(pads_zeroed, 1)
            nc.gpsimd.memset(wv_sb[:, D:VW], 1.0).then_inc(pads_zeroed, 1)
            nc.gpsimd.memset(shift_sb[:], SHIFT).then_inc(consts_ready, 1)
            nc.gpsimd.memset(blockmask[:], 1.0).then_inc(mask_step, 1)
            pool.wait_ge(mask_step, 1)
            for s in range(SLOTS):
                part = blockmask[32 * s:32 * s + 32, :]
                nc.gpsimd.affine_select(out=part, in_=part, compare_op=ALU.is_ge, fill=0.0, base=0,
                                        pattern=[[-DH, QUAD]], channel_multiplier=1).then_inc(mask_step, 1)
            pool.wait_ge(mask_step, 1 + SLOTS)
            for s in range(SLOTS):
                part = blockmask[32 * s:32 * s + 32, :]
                nc.gpsimd.affine_select(out=part, in_=part, compare_op=ALU.is_ge, fill=0.0, base=DH - 1,
                                        pattern=[[DH, QUAD]], channel_multiplier=-1).then_inc(mask_step, 1)
            pool.wait_ge(mask_step, 1 + 2 * SLOTS)
            nc.gpsimd.memset(ident[:], 0.0).then_inc(ident_ready, 1)
            pool.wait_ge(ident_ready, 1)
            nc.gpsimd.affine_select(out=ident[:], in_=ident[:], compare_op=ALU.not_equal, fill=1.0, base=0,
                                    pattern=[[-1, P]], channel_multiplier=1).then_inc(ident_ready, 1)
            pool.wait_ge(ident_ready, 2)
            nc.gpsimd.memset(values[:, 0, :, :, PAIR * DH + 1:], 0.0).then_inc(values_zeroed, 1)
            nc.gpsimd.memset(k_parts[:, :, :, SK:SKP].bitcast(F32), 0.0).then_inc(pads_zeroed, 1)
            nc.gpsimd.memset(head_sum[:], 1.0).then_inc(selectors_ready, 1)
            pool.wait_ge(selectors_ready, 1)
            nc.gpsimd.affine_select(out=head_sum[:], in_=head_sum[:], compare_op=ALU.is_ge, fill=0.0, base=0,
                                    pattern=[[-DH, HEADS]], channel_multiplier=1).then_inc(selectors_ready, 1)
            pool.wait_ge(selectors_ready, 2)
            nc.gpsimd.affine_select(out=head_sum[:], in_=head_sum[:], compare_op=ALU.is_ge, fill=0.0,
                                    base=DH - 1, pattern=[[DH, HEADS]], channel_multiplier=-1
                                    ).then_inc(selectors_ready, 1)
            pool.wait_ge(selectors_ready, 3)
            nc.gpsimd.memset(ones[:], 1.0).then_inc(selectors_ready, 1)
            pool.wait_ge(q_projected, QGROUPS)
            nc.gpsimd.memset(values[:, 1, :, :, PAIR * DH + 1:], 0.0).then_inc(values_zeroed, 1)
            for part, source, slots in ((0, q_high, (0, 1)), (1, q_low, (2, 3))):
                pool.wait_ge(q_split, 3 + part)
                for t in range(QUADS):
                    for s in slots:
                        pool.dma_start(
                            query_rep[32 * s:32 * s + 32, t, QB * SQ:].rearrange(
                                "p (g n) -> p g n", n=QB * SQ).bitcast(F32),
                            source[32 * t:32 * t + 32, 1:, :].bitcast(F32)).then_inc(q_replicated, 16)
        @block.scalar
        def _(act):
            act.dma_start(wq_sb[:], Wq).then_inc(wq_loaded, 16)
            act.dma_start(bq_sb[:], bq).then_inc(wq_loaded, 16)
            act.dma_start(xT_sb[:, 0:QB * SQ].rearrange("p (b q) -> p b q", b=QB), xT[:, 0:QB, :]
                          ).then_inc(first_xT_loaded, 16)
            for part, source, slots in ((1, q_high, (0, 1)), (2, q_low, (2, 3))):
                act.wait_ge(q_split, part)
                for t in range(QUADS):
                    for s in slots:
                        act.dma_start(query_rep[32 * s:32 * s + 32, t, 0:QB * SQ].bitcast(F32),
                                      source[32 * t:32 * t + 32, 0, :].bitcast(F32)
                                      ).then_inc(first_q_replicated, 16)
            act.wait_ge(consts_ready, 1)

            def batch(b, parity):
                for u in range(UNITS):
                    act.wait_ge(scores_ready, UNITS * b + u + 1)
                    if not isinstance(b, int) or b > 0 or u >= PROB_SLOTS:
                        act.wait_ge(pv_done, UNITS * b + u + 1 - PROB_SLOTS)
                    nc.scalar.activation(probs[:, u % PROB_SLOTS], scores_ps[:, u % SCORE_SLOTS, :, 0:QCOLS],
                                         ACT.Exp, bias=shift_sb[:], scale=SCALE).then_inc(probs_ready, 1)

            batch(0, 0)
            pairs_loop(act, 1, B - 1, batch)
            batch(B - 1, 1)

            def general(b):
                with nc.Fori(0, HEADS, engines=[act.engine]) as h:
                    n = b * HEADS + h
                    act.wait_ge(g_masked, 4 * n + 4)
                    nc.scalar.activation(g_scores[:, 0:SK], g_scores[:, 0:SK], ACT.Exp, bias=g_stat[:, 1:2],
                                         accum_out=g_stat[:, 2:3]).then_inc(g_exped, 1)

            general_path(act, general)

        @block.tensor
        def _(pe):
            def work(index):
                if not isinstance(index, int) or index > 0:
                    pe.wait_ge(work_free, index)

            def project_keys(bank, parity, c, part, parts):
                end = min((c + 1) * BANK, SK)
                step = BANK // parts
                at, to = c * BANK + part * step, min(c * BANK + (part + 1) * step, end)
                return nc.tensor.matmul(bank[:, at - c * BANK:to - c * BANK], wk_sb[:], keyT[:, parity, at:to],
                                        start=True, stop=True)

            def project_values(bank, parity, g, n):
                kt = g * VGROUP + n
                return nc.tensor.matmul(bank[:, n * VW:(n + 1) * VW], keyT[:, parity, kt * P:(kt + 1) * P],
                                        wv_sb[:], start=True, stop=True)

            def transpose_outputs():
                for n in range(HALVES * PAIR):
                    mm = nc.tensor.transpose(work_ps[0:SQ, n * P:(n + 1) * P], o_sb[:, n * SQ:(n + 1) * SQ],
                                             ident[:])
                return mm

            def prepare(b, parity, k, piece, index):
                if k == 0 and piece == 0:
                    pe.wait_ge(key_loaded[parity], 8 * (b - parity) + 16 * parity)
                if piece == 0:
                    work(index)
                if k < KCHUNKS:
                    mm = project_keys(work_ps, parity, k, piece, KPIECES)
                else:
                    mm = project_values(work_ps, parity, k - KCHUNKS, piece)
                if piece == (KPIECES if k < KCHUNKS else VGROUP) - 1:
                    mm.then_inc(work_filled, 1)

            def scores(b, parity, u):
                kt, half = divmod(u, HALVES)
                if u == 0:
                    pe.wait_ge(k_replicated, 16 * REPLICAS * (b + 1))
                    pe.wait_ge(qbd_ready, b + 1)
                if not isinstance(b, int) or b > 0 or u >= SCORE_SLOTS:
                    pe.wait_ge(probs_ready, UNITS * b + u + 1 - SCORE_SLOTS)
                for n in range(HALF_QUADS):
                    t = half * HALF_QUADS + n
                    mm = nc.tensor.matmul(scores_ps[:, u % SCORE_SLOTS, n, 0:QCOLS],
                                          k_parts[:, parity, t, kt * P:(kt + 1) * P],
                                          query_bd[:, parity, t, :], start=True, stop=True)
                mm.then_inc(scores_ready, 1)

            def value_products(b, parity, u):
                kt, half = divmod(u, HALVES)
                if u == 0:
                    pe.wait_ge(v_ready, (KT + 1) * (b + 1))
                    if not isinstance(b, int) or b > 0:
                        pe.wait_ge(o_copied, b)
                pe.wait_ge(probs_ready, UNITS * b + u + 1)
                for c in range(HALF_PAIRS):
                    n, off = divmod(c * PCOLS, QCOLS)
                    mm = nc.tensor.matmul(
                        o_ps[c * VCOLS:(c + 1) * VCOLS, half * PCOLS:(half + 1) * PCOLS],
                        values[:, parity, kt, half * HALF_PAIRS + c, :],
                        probs[:, u % PROB_SLOTS, n, off:off + PCOLS],
                        start=(u == 0), stop=(kt == KT - 1), skip_group_check=True)
                mm.then_inc(pv_done, 1)

            PLACES = {}
            OUTPUTS = (-1, 0)

            def place_step(k, *places):
                for piece, place in enumerate(places):
                    PLACES[place] = (k, piece)

            place_step(0, (0, 0), (0, 2))
            place_step(1, (1, 1), (1, 2))
            place_step(2, (2, 1), (2, 2))
            place_step(-1, (4, 0))
            place_step(KCHUNKS + 0, (5, 0), (5, 1), (5, 2))
            place_step(KCHUNKS + 1, (6, 2), (7, 0), (7, 1))
            place_step(KCHUNKS + 2, (8, 1), (8, 2), (9, 0))
            place_step(KCHUNKS + 3, (10, 0), (10, 1), (10, 2))

            def batch(b, parity, first=False, last=False):
                used = works_before(b)

                def side_work(place):
                    nonlocal used
                    step = PLACES.get((kt, place))
                    if step == OUTPUTS:
                        if not first:
                            work(used)
                            pe.wait_ge(o_copied, b)
                            transpose_outputs().then_inc(work_filled, 1)
                            used = used + 1
                    elif step and not last:
                        k, piece = step
                        prepare(b + 1, 1 - parity, k, piece, used)
                        if piece == (KPIECES if k < KCHUNKS else VGROUP) - 1:
                            used = used + 1

                for kt in range(KT):
                    side_work(0)
                    for half in range(HALVES):
                        u = kt * HALVES + half
                        if u + LEAD < UNITS:
                            scores(b, parity, u + LEAD)
                        elif not last:
                            scores(b + 1, 1 - parity, u + LEAD - UNITS)
                        side_work(1 + half)
                    if last and kt == KT // 2:
                        check_batches(used)
                    for half in range(HALVES):
                        value_products(b, parity, kt * HALVES + half)
                return used

            def check_batches(used):
                pe.wait_ge(selectors_ready, 4)
                work(used)
                pe.wait_ge(bound_made, B)
                nc.tensor.matmul(work_ps[0:B, 0:HEADS], bound_terms[:], head_sum[:], start=True, stop=True)
                pe.wait_ge(kept_counted, B)
                nc.tensor.matmul(work_ps[0:B, HEADS:HEADS + 1], kept_keys[:], ones[:, 0:1],
                                 start=True, stop=True).then_inc(checks_summed, 1)
                pe.wait_ge(check_step, 4)
                nc.tensor.matmul(work_ps[0:1, 0:1], batch_checks[:, 3:4], ones[0:B, 0:1],
                                 start=True, stop=True).then_inc(checks_summed, 1)

            banks = scores_ps[:].rearrange("p a b c -> p (a b) c")

            def project_queries(g):
                nc.tensor.matmul(banks[:, Q_BANKS[g], 0:QB * SQ], wq_sb[:], xT_sb[:, g * QB * SQ:(g + 1) * QB * SQ],
                                 start=True, stop=True).then_inc(q_projected, 1)

            pe.wait_ge(wq_loaded, 32)
            pe.wait_ge(first_xT_loaded, 16)
            project_queries(0)
            pe.wait_ge(wk_loaded, 32)
            for c in range(KCHUNKS):
                pe.wait_ge(first_keys_loaded[c], 16)
                if K_BANKS[c] == Q_BANKS[0]:
                    pe.wait_ge(q_relued, 1)
                project_keys(banks[:, K_BANKS[c], :], 0, c, 0, 1).then_inc(first_projected, 1)
            pe.wait_ge(xT_loaded, 16)
            for g in range(1, QGROUPS):
                project_queries(g)
            pe.wait_ge(wv_loaded, 32)
            pe.wait_ge(pads_zeroed, 2)
            pe.wait_ge(first_evacuated, KCHUNKS)
            pe.wait_ge(q_relued, QGROUPS)
            for g in range(VGROUPS):
                for n in range(VGROUP):
                    mm = project_values(banks[:, V_BANKS[g], :], 0, g, n)
                mm.then_inc(first_projected, 1)
            pe.wait_ge(first_evacuated, KCHUNKS + VGROUPS)
            pe.wait_ge(pads_zeroed, 3)
            pe.wait_ge(ident_ready, 2)
            for u in range(LEAD):
                scores(0, 0, u)
            batch(0, 0, first=True)
            pairs_loop(pe, 1, B - 1, batch)
            used = batch(B - 1, 1, last=True)
            pe.wait_ge(path_chosen, 1)
            pe.wait_ge(o_copied, B)
            transpose_outputs().then_inc(work_filled, 1)

            banks = scores_ps[:].rearrange("p a b c -> p (a b) c")

            def general(b):
                pe.wait_ge(g_loaded, 16 * (b + 1))
                for c in range(KCHUNKS):
                    nc.tensor.matmul(banks[:, c, :], wk_sb[:], keyT[:, 0, c * BANK:(c + 1) * BANK],
                                     start=True, stop=True)
                    nc.tensor.matmul(banks[:, KCHUNKS + c, :], ones[:], keyT[:, 0, c * BANK:(c + 1) * BANK],
                                     start=True, stop=True).then_inc(g_projected, 1)
                pe.wait_ge(g_keys_made, 3 * (b + 1))
                for kt in range(KT):
                    c, n = divmod(kt, BANK // P)
                    nc.tensor.matmul(banks[:, c, n * P:(n + 1) * P], keyT[:, 0, kt * P:(kt + 1) * P],
                                     wv_sb[:, 0:D], start=True, stop=True).then_inc(g_values_projected, 1)
                with nc.Fori(0, HEADS, engines=[pe.engine]) as h:
                    n = b * HEADS + h
                    pe.wait_ge(g_prepared, 2 * (b + 1))
                    pe.wait_ge(g_query_made, n + 1)
                    for c in range(KCHUNKS):
                        mm = nc.tensor.matmul(banks[0:SQ, c, :], g_query, g_keys[:, c * BANK:(c + 1) * BANK],
                                              start=True, stop=True)
                    mm.then_inc(g_scored, 1)
                    pe.wait_ge(g_exped, n + 1)
                    for kt in range(KT):
                        c, m = divmod(kt, BANK // P)
                        mm = nc.tensor.transpose(banks[:, KCHUNKS + c, m * P:m * P + SQ],
                                                 g_scores[:, kt * P:(kt + 1) * P], ident[0:SQ, 0:SQ])
                    mm.then_inc(g_transposed, 1)
                    pe.wait_ge(g_copied, n + 1)
                    for kt in range(KT):
                        mm = nc.tensor.matmul(work_ps[0:SQ, 0:DH], g_probsT[:, kt, 0:SQ],
                                              g_values[:, kt, bass.ds(h * DH, DH)],
                                              start=(kt == 0), stop=(kt == KT - 1))
                    mm.then_inc(g_summed, 1)

            general_path(pe, general)

        @block.vector
        def _(dve):
            v = nc.vector
            banks = scores_ps[:].rearrange("p a b c -> p (a b) c")

            def read_keys(b, k0, before=True):
                for c in range(KCHUNKS):
                    end = min((c + 1) * BANK, SK)
                    filled, free, bank = (work_filled, work_free, work_ps) if before else \
                        (first_projected, first_evacuated, banks[:, K_BANKS[c], :])
                    dve.wait_ge(filled, k0 + c + 1)
                    if c == 0 and before:
                        dve.wait_ge(k_low_ready, b)
                    v.tensor_scalar(k_raw[:, c * BANK:end], bank[:, 0:end - c * BANK], bk_sb[:], None,
                                    ALU.add, ALU.max, accum_out=k_chunk_max[:, c:c + 1]).then_inc(free, 1)

            def high_keys(b, parity, k0, before=True):
                dve.wait_ge(work_free if before else first_evacuated, k0 + KCHUNKS)
                v.tensor_reduce(k_max[:, parity:parity + 1], k_chunk_max[:], AX.X, ALU.max).then_inc(k_max_ready, 1)
                dve.wait_ge(k_max_ready, 2 * b + 1)
                v.tensor_scalar(k_max[:, parity:parity + 1], k_max[:, parity:parity + 1], 0.0, None, ALU.max).then_inc(k_max_ready, 1)
                dve.wait_ge(k_max_ready, 2 * b + 2)
                if before:
                    dve.wait_ge(k_replicated, 16 * REPLICAS * b)
                v.tensor_scalar(k_high[:], k_raw[:, 0:SK], 0.0, k_max[:, parity:parity + 1], ALU.max, ALU.subtract
                                ).then_inc(k_high_ready, 1)

            def low_keys(b, parity):
                v.tensor_scalar(k_cent[:, 0:SK], k_raw[:, 0:SK], 0.0, k_max[:, parity:parity + 1], ALU.max, ALU.subtract
                                ).then_inc(k_cent_ready, 1)
                dve.wait_ge(k_high_ready, b + 1)
                dve.wait_ge(k_cent_ready, b + 1)
                v.tensor_tensor(k_low[:], k_cent[:, 0:SK], k_high[:].bitcast(F32), ALU.subtract
                                ).then_inc(k_low_ready, 1)

            def bound_scores(b, parity):
                at = slice(b, b + 1) if isinstance(b, int) else bass.ds(b, 1)
                v.tensor_tensor(bound_terms[:, at], k_max[:, parity:parity + 1], q_max[:, at], ALU.mult
                                ).then_inc(bound_made, 1)

            def finish_values(b, parity, g, index, before=True):
                rows = slice(g * VGROUP, (g + 1) * VGROUP)
                filled, free, bank = (work_filled, work_free, work_ps) if before else \
                    (first_projected, first_evacuated, banks[:, V_BANKS[g], :])
                dve.wait_ge(filled, index + 1)
                work = bank[:, 0:VGROUP * VW].rearrange("p (n w) -> p n w", w=VW)
                v.tensor_scalar(keep[:, rows], work[:, :, D], 0.0, None, ALU.not_equal).then_inc(keep_ready, 1)
                v.tensor_tensor(v_biased[:, g % 2], work[:, :, 0:D],
                                bv_sb[:].unsqueeze(1).to_broadcast([P, VGROUP, D]), ALU.add
                                ).then_inc(free, 1)
                dve.wait_ge(keep_ready, VGROUPS * b + g + 1)
                dve.wait_ge(free, index + 1)
                for n in range(VGROUP):
                    kt = g * VGROUP + n
                    v.tensor_scalar(values[:, parity, kt, :, 0:PAIR * DH],
                                    v_biased[:, g % 2, n].rearrange("p (a w) -> p a w", w=PAIR * DH),
                                    0.0, keep[:, kt:kt + 1], ALU.max, ALU.mult).then_inc(v_ready, 1)

            def finish_keep(b, parity):
                v.tensor_copy(values[:, parity, :, :, PAIR * DH],
                              keep[:].unsqueeze(2).to_broadcast([P, KT, PAIRS])).then_inc(v_ready, 1)
                at = slice(b, b + 1) if isinstance(b, int) else bass.ds(b, 1)
                v.tensor_reduce(kept_keys[:, at], keep[:], AX.X, ALU.add).then_inc(kept_counted, 1)

            def spread_queries(b, parity):
                src = query_rep[:, :, b * SQ:(b + 1) * SQ] if isinstance(b, int) else \
                    query_rep[:, :, bass.ds(b * SQ, SQ)]
                for t in range(QUADS):
                    ins = v.tensor_tensor(
                        query_bd[:, parity, t, :].rearrange("p (h q) -> p h q", h=QUAD),
                        src[:, t].bitcast(F32).unsqueeze(1).to_broadcast([P, QUAD, SQ]),
                        blockmask[:].unsqueeze(2).to_broadcast([P, QUAD, SQ]), ALU.mult)
                ins.then_inc(qbd_ready, 1)

            def copy_outputs(b):
                dve.wait_ge(pv_done, UNITS * (b + 1))
                v.tensor_copy(o_sb[:], o_ps[:, 0:HALVES * PCOLS]).then_inc(o_copied, 1)

            def finish_outputs(b, index):
                dve.wait_ge(work_filled, index + 1)
                t = work_ps[0:SQ, :].rearrange("q (rj c w) -> q rj c w", c=HALF_PAIRS, w=VCOLS)
                v.tensor_scalar(inv_den[:], t[:, :, :, PAIR * DH], DEN_FLOOR, None, ALU.max).then_inc(den_read, 1)
                dve.wait_ge(den_read, b + 1)
                v.reciprocal(inv_den[:], inv_den[:]).then_inc(den_inverted, 1)
                dve.wait_ge(den_inverted, b + 1)
                o = o_norm[:].rearrange("q (r c j d) -> q r c j d", r=HALVES, c=HALF_PAIRS, j=PAIR)
                t = work_ps[0:SQ, :].rearrange("q (r j c w) -> q r j c w", r=HALVES, j=PAIR, w=VCOLS)
                i = inv_den[:].rearrange("q (r j) c -> q r j c", j=PAIR)
                for j, done in ((0, o_half_normed), (1, work_free)):
                    v.tensor_tensor(o[:, :, :, j, :], t[:, :, j, :, j * DH:(j + 1) * DH],
                                    i[:, :, j, :].unsqueeze(3).to_broadcast([SQ, HALVES, HALF_PAIRS, DH]),
                                    ALU.mult).then_inc(done, 1)
                dve.wait_ge(o_half_normed, b + 1)
                dve.wait_ge(work_free, index + 1)
                at = slice(b, b + 1) if isinstance(b, int) else bass.ds(b, 1)
                v.scalar_tensor_tensor(out=out_sb[:, at, :].rearrange("q a d -> q (a d)"), in0=o_norm[:],
                                       scalar=q_mask[:, at], in1=x_sb[:, at, :].rearrange("q a d -> q (a d)"),
                                       op0=ALU.mult, op1=ALU.add).then_inc(out_ready, 1)

            def batch(b, parity, first=False, last=False):
                used = works_before(b)
                if not first:
                    copy_outputs(b - 1)
                if not last:
                    read_keys(b + 1, used)
                    high_keys(b + 1, 1 - parity, used)
                    used = used + KCHUNKS
                if not first:
                    finish_outputs(b - 1, used)
                    used = used + 1
                if not last:
                    low_keys(b + 1, 1 - parity)
                    if first:
                        reduce_queries()
                        bound_scores(b, parity)
                        dve.wait_ge(values_zeroed, 2)
                    bound_scores(b + 1, 1 - parity)
                    finish_values(b + 1, 1 - parity, 0, used)
                    spread_queries(b + 1, 1 - parity)
                    for g in range(1, VGROUPS):
                        finish_values(b + 1, 1 - parity, g, used + g)
                    finish_keep(b + 1, 1 - parity)
                    used = used + VGROUPS
                return used

            def reduce_queries():
                dve.wait_ge(x_loaded, 16)
                v.tensor_reduce(q_sum[:], x_sb[:], AX.X, ALU.add).then_inc(q_masked, 1)
                dve.wait_ge(q_masked, 1)
                v.tensor_scalar(q_mask[:], q_sum[:], 0.0, None, ALU.not_equal).then_inc(q_masked, 1)
                v.tensor_reduce(q_max[:], queryT[:].rearrange("p (b q) -> p b q", b=B), AX.X, ALU.max
                                ).then_inc(q_masked, 1)
                dve.wait_ge(q_masked, 3)

            def split_queries(first, last):
                for g in range(first, last):
                    dve.wait_ge(q_projected, g + 1)
                    v.tensor_scalar(queryT[:, g * QB * SQ:(g + 1) * QB * SQ],
                                    scores_ps[:].rearrange("p a b c -> p (a b) c")[:, Q_BANKS[g], 0:QB * SQ],
                                    bq_sb[:], 0.0, ALU.add, ALU.max).then_inc(q_relued, 1)
                dve.wait_ge(q_relued, last)
                relued = queryT[:, first * QB * SQ:last * QB * SQ].rearrange("p (g n) -> p g n", n=QB * SQ)
                part = 1 if first == 0 else 3
                v.tensor_copy(q_high[:, first:last, :], relued).then_inc(q_split, 1)
                dve.wait_ge(q_split, part)
                v.tensor_tensor(q_low[:, first:last, :], relued, q_high[:, first:last, :].bitcast(F32),
                                ALU.subtract).then_inc(q_split, 1)

            dve.wait_ge(wk_loaded, 32)
            dve.wait_ge(wq_loaded, 32)
            split_queries(0, 1)
            read_keys(0, 0, False)
            high_keys(0, 0, 0, False)
            low_keys(0, 0)
            split_queries(1, QGROUPS)
            dve.wait_ge(wv_loaded, 32)
            dve.wait_ge(values_zeroed, 1)
            for g in range(VGROUPS):
                finish_values(0, 0, g, KCHUNKS + g, False)
            finish_keep(0, 0)
            dve.wait_ge(mask_step, 1 + 2 * SLOTS)
            dve.wait_ge(first_q_replicated, 16 * REPLICAS)
            spread_queries(0, 0)
            batch(0, 0, first=True)
            pairs_loop(dve, 1, B - 1, batch)
            used = batch(B - 1, 1, last=True)

            dve.wait_ge(checks_summed, 1)
            v.tensor_reduce(batch_checks[:, 0:1], work_ps[0:B, 0:HEADS], AX.X, ALU.max).then_inc(check_step, 1)
            v.tensor_scalar(batch_checks[:, 2:3], work_ps[0:B, HEADS:HEADS + 1], 0.5, None, ALU.is_ge
                            ).then_inc(check_step, 1)
            dve.wait_ge(check_step, 2)
            v.tensor_scalar(batch_checks[:, 1:2], batch_checks[:, 0:1], BOUND_LIMIT / SCALE, None, ALU.is_le
                            ).then_inc(check_step, 1)
            dve.wait_ge(check_step, 3)
            v.tensor_tensor(batch_checks[:, 3:4], batch_checks[:, 1:2], batch_checks[:, 2:3], ALU.mult
                            ).then_inc(check_step, 1)
            dve.wait_ge(checks_summed, 2)
            v.tensor_copy(bounded[:], work_ps[0:1, 0:1]).then_inc(path_chosen, 1)
            copy_outputs(B - 1)
            finish_outputs(B - 1, used)

            banks = scores_ps[:].rearrange("p a b c -> p (a b) c")

            def flat(ap, parts=P):
                return ap.rearrange("p (c n) -> p c n", n=BANK)

            def general(b):
                at = bass.ds(b, 1)
                dve.wait_ge(g_projected, KCHUNKS * (b + 1))
                v.tensor_scalar(flat(g_keys[:]), banks[:, 0:KCHUNKS, :], bk_sb[:], 0.0, ALU.add, ALU.max
                                ).then_inc(g_keys_made, 1)
                v.tensor_scalar(flat(g_keep[:]), banks[:, KCHUNKS:2 * KCHUNKS, :], 0.0, None, ALU.not_equal
                                ).then_inc(g_keys_made, 1)
                dve.wait_ge(g_keys_made, 3 * b + 2)
                v.tensor_scalar(g_mask, g_keep[:], -1.0, NEG, ALU.add, ALU.mult).then_inc(g_keys_made, 1)
                dve.wait_ge(g_values_projected, KT * (b + 1))
                for c in range(KCHUNKS):
                    n = BANK // P
                    ins = v.tensor_tensor(g_values[:, c * n:(c + 1) * n, :],
                                          banks[:, c, :].rearrange("p (n w) -> p n w", w=D),
                                          bv_sb[:].unsqueeze(1).to_broadcast([P, n, D]), ALU.add)
                ins.then_inc(g_prepared, 1)
                dve.wait_ge(g_prepared, 2 * b + 1)
                v.tensor_scalar(g_values, g_values, 0.0, None, ALU.max).then_inc(g_prepared, 1)
                with nc.Fori(0, HEADS, engines=[dve.engine]) as h:
                    n = b * HEADS + h
                    dve.wait_ge(g_keys_made, 3 * (b + 1))
                    v.tensor_scalar(g_query, queryT[:, bass.ds(b * SQ, SQ)], head_sum[:, bass.ds(h, 1)], None,
                                    ALU.mult).then_inc(g_query_made, 1)
                    dve.wait_ge(g_scored, n + 1)
                    v.scalar_tensor_tensor(out=flat(g_scores, SQ), in0=banks[0:SQ, 0:KCHUNKS, :], scalar=SCALE,
                                           in1=flat(g_keep[0:SQ, :]), op0=ALU.mult, op1=ALU.mult
                                           ).then_inc(g_masked, 1)
                    dve.wait_ge(g_masked, 4 * n + 1)
                    v.tensor_tensor(g_scores, g_scores, g_mask[0:SQ], ALU.add).then_inc(g_masked, 1)
                    dve.wait_ge(g_masked, 4 * n + 2)
                    v.tensor_reduce(g_stat[:, 0:1], g_scores[:, 0:SK], AX.X, ALU.max).then_inc(g_masked, 1)
                    dve.wait_ge(g_masked, 4 * n + 3)
                    v.memset(g_scores[:, SK:SKP], 0.0)
                    v.tensor_scalar(g_stat[:, 1:2], g_stat[:, 0:1], -1.0, None, ALU.mult).then_inc(g_masked, 1)
                    dve.wait_ge(g_exped, n + 1)
                    v.reciprocal(g_stat[:, 3:4], g_stat[:, 2:3]).then_inc(g_inverted, 1)
                    dve.wait_ge(g_transposed, n + 1)
                    for c in range(KCHUNKS):
                        m = BANK // P
                        ins = v.tensor_copy(g_probsT[:, c * m:(c + 1) * m, 0:SQ],
                                            banks[:, KCHUNKS + c, :].rearrange("p (n q) -> p n q", q=P)[:, :, 0:SQ])
                    ins.then_inc(g_copied, 1)
                    dve.wait_ge(g_summed, n + 1)
                    dve.wait_ge(g_inverted, n + 1)
                    v.tensor_scalar(g_out[:, bass.ds(h * DH, DH)], work_ps[0:SQ, 0:DH], g_stat[:, 3:4], None,
                                    ALU.mult).then_inc(g_head_done, 1)
                dve.wait_ge(g_head_done, HEADS * (b + 1))
                v.scalar_tensor_tensor(out=g_out[:], in0=g_out[:], scalar=q_mask[:, at],
                                       in1=x_sb[:, at, :].rearrange("q a d -> q (a d)"),
                                       op0=ALU.mult, op1=ALU.add).then_inc(g_out_made, 1)
                dve.wait_ge(g_stored, 16 * (b + 1))

            general_path(dve, general)


def kernel(**inputs):
    import numpy as np
    import concourse.bacc as bacc
    from concourse.bass_utils import run_bass_kernel_spmd

    a = {name: np.asarray(value) for name, value in inputs.items()}
    arrays = {
        "x": a["x"],
        "xT": np.ascontiguousarray(a["x"].transpose(2, 0, 1)),
        "ctxT": np.ascontiguousarray(a["ctx_1024"].transpose(0, 2, 1)),
        "Wq": a["L0_xattn_Wq"],
        "bq": a["L0_xattn_bq"].reshape(-1, 1),
        "Wk": a["L0_xattn_Wk"],
        "bk": a["L0_xattn_bk"].reshape(-1, 1),
        "Wv": a["L0_xattn_Wv"],
        "bv": a["L0_xattn_bv"].reshape(1, -1),
    }
    nc = bacc.Bacc("TRN2", target_bir_lowering=False, num_devices=1)
    args = [nc.dram_tensor(f"in_{name}", value.shape, mybir.dt.from_np(value.dtype), kind="ExternalInput").ap()
            for name, value in arrays.items()]
    args.append(nc.dram_tensor("out", a["x"].shape, F32, kind="ExternalOutput").ap())
    attention(nc, *args)
    r = run_bass_kernel_spmd(nc, [{f"in_{name}": value for name, value in arrays.items()}], core_ids=[0])
    return r.results[0]["out"]
```

```python
from contextlib import ExitStack

import concourse.bass as bass
from concourse import mybir

F32 = mybir.dt.float32
F32R = mybir.dt.float32r
I32 = mybir.dt.int32
ALU = mybir.AluOpType
ACT = mybir.ActivationFunctionType
AX = mybir.AxisListType

P = 128
BANK = 512

SLOTS = 4
HEADS = 16
QUAD = 4
PAIR = 2
VCOLS = 32
SCORE_SLOTS = 3
PROB_SLOTS = 4
LEAD = 2
SHIFT = 40.0
BOUND_LIMIT = 100.0
DEN_FLOOR = 1e-30
NEG = float(2 ** 32)


def attention(
    nc: bass.Bass,
    x: bass.AP,
    xT: bass.AP,
    ctxT: bass.AP,
    Wq: bass.AP,
    bq: bass.AP,
    Wk: bass.AP,
    bk: bass.AP,
    Wv: bass.AP,
    bv: bass.AP,
    out: bass.AP,
):
    B, SQ, D = x.shape
    SK = ctxT.shape[2]
    DH = D // HEADS
    SCALE = 1.0 / DH ** 0.5
    KT = -(-SK // P)
    SKP = KT * P
    QUADS = HEADS // QUAD
    PAIRS = HEADS // PAIR
    HALVES = 2
    HALF_PAIRS = PAIRS // HALVES
    HALF_QUADS = QUADS // HALVES
    UNITS = KT * HALVES
    QCOLS = QUAD * SQ
    PCOLS = PAIR * SQ
    VW = D + 1
    VGROUP = 3
    VGROUPS = KT // VGROUP
    KCHUNKS = SKP // BANK
    QB = 4
    QGROUPS = B // QB
    assert D == P and DH * QUAD == 32 and VGROUP * VW <= BANK and HALF_PAIRS * VCOLS == P
    assert UNITS % SCORE_SLOTS == 0 and UNITS % PROB_SLOTS == 0 and B % 2 == 0 and B % QB == 0
    assert QB * SQ <= BANK and 2 * QB * SQ <= SK and QGROUPS <= QUADS and QCOLS <= BANK and HALVES * PCOLS <= BANK
    KPIECES = 2
    Q_BANKS = (0, 5, 6, 7)
    K_BANKS = (1, 2, 3)
    V_BANKS = (1, 2, 3, 0)
    Q_SPREAD_BANK = 4
    K_SPREAD_BANKS = (4, 5, 6, 7)
    REPLICAS = SLOTS * QUADS
    Q_HIGH_AT, Q_LOW_AT, K_HIGH_AT, K_LOW_AT, SELECTOR_SLOTS = 0, 2, 6, 7, 11

    ctx = ExitStack()
    with ctx:
        def sb(name, shape, dt=F32):
            return ctx.enter_context(nc.sbuf_tensor(name, shape, dt))

        def sem(name):
            return ctx.enter_context(nc.semaphore(name))

        wq_sb = sb("wq_sb", [P, D])
        wk_sb = sb("wk_sb", [P, D])
        wv_sb = sb("wv_sb", [P, VW])
        bq_sb = sb("bq_sb", [P, 1])
        bk_sb = sb("bk_sb", [P, 1])
        bv_sb = sb("bv_sb", [P, D])
        ident = sb("ident", [P, P])
        blockmask = sb("blockmask", [P, QUAD])
        selectors = sb("selectors", [P, QUADS, SELECTOR_SLOTS, 32], F32R)
        shift_sb = sb("shift_sb", [P, 1])
        keyT = sb("keyT", [P, 2, SKP])
        queryT = sb("queryT", [P, B * SQ])
        query_rep = sb("query_rep", [P, QUADS, B * SQ], F32R)
        query_bd = sb("query_bd", [P, 2, QUADS, QCOLS], F32R)
        k_raw = sb("k_raw", [P, SKP])
        k_cent = sb("k_cent", [P, SKP])
        k_high = sb("k_high", [P, SK], F32R)
        k_low = sb("k_low", [P, SK], F32R)
        k_parts = sb("k_parts", [P, 2, QUADS, SKP], F32R)
        k_chunk_max = sb("k_chunk_max", [P, KCHUNKS])
        k_max = sb("k_max", [P, 2])
        v_biased = sb("v_biased", [P, 2, VGROUP, D])
        keep = sb("keep", [P, KT])
        values = sb("values", [P, 2, KT, PAIRS, VCOLS])
        probs = sb("probs", [P, PROB_SLOTS, HALF_QUADS, QCOLS])
        o_sb = sb("o_sb", [P, HALVES * PCOLS])
        inv_den = sb("inv_den", [SQ, HALVES * PAIR, HALF_PAIRS])
        o_norm = sb("o_norm", [SQ, D])
        x_sb = sb("x_sb", [SQ, B, D])
        q_sum = sb("q_sum", [SQ, B])
        q_mask = sb("q_mask", [SQ, B])
        out_sb = sb("out_sb", [SQ, B, D])
        q_max = sb("q_max", [P, B])

        head_sum = sb("head_sum", [P, HEADS])
        ones = sb("ones", [P, P])
        bound_terms = sb("bound_terms", [P, B])
        kept_keys = sb("kept_keys", [P, B])
        batch_checks = sb("batch_checks", [B, 4])
        bounded = sb("bounded", [1, 1], I32)

        g_keys = k_raw
        g_keep = k_cent
        g_values = values[:, 0].rearrange("p a b c -> p (a b c)")[:, 0:KT * D].rearrange("p (n w) -> p n w", w=D)
        g_mask = probs[:].rearrange("p a b c -> p (a b c)")[:, 0:SKP]
        g_scores = probs[:].rearrange("p a b c -> p (a b c)")[0:SQ, SKP:2 * SKP]
        g_probsT = values[:, 1].rearrange("p a b c -> p (a b c)")[:, 0:KT * P].rearrange("p (n q) -> p n q", q=P)
        g_query = o_sb[:, 0:SQ]
        g_out = o_norm
        g_stat = sb("g_stat", [SQ, 4])

        xT_sb = values[:, 1].rearrange("p a b c -> p (a b c)")[:, 0:B * SQ]
        q_high = k_parts[:, 1, 0:QGROUPS, 0:QB * SQ]
        q_low = k_parts[:, 1, 0:QGROUPS, QB * SQ:2 * QB * SQ]

        psum = ctx.enter_context(nc.psum_tensor("psum", [P, SCORE_SLOTS * HALF_QUADS + 2, BANK], F32))
        scores_ps = psum[:, 0:SCORE_SLOTS * HALF_QUADS, :].rearrange("p (a b) c -> p a b c", b=HALF_QUADS)
        o_ps = psum[:, SCORE_SLOTS * HALF_QUADS, :]
        work_ps = psum[:, SCORE_SLOTS * HALF_QUADS + 1, :]

        first_xT_loaded = sem("first_xT_loaded")
        xT_loaded = sem("xT_loaded")
        wq_loaded = sem("wq_loaded")
        bq_loaded = sem("bq_loaded")
        bk_loaded = sem("bk_loaded")
        wk_loaded = sem("wk_loaded")
        wv_loaded = sem("wv_loaded")
        x_loaded = sem("x_loaded")
        first_keys_loaded = [sem(f"first_keys_loaded{c}") for c in range(KCHUNKS)]
        key_loaded = [sem("even_keys_loaded"), sem("odd_keys_loaded")]
        pads_zeroed = sem("pads_zeroed")
        consts_ready = sem("consts_ready")
        values_zeroed = sem("values_zeroed")
        ident_ready = sem("ident_ready")
        mask_step = sem("mask_step")
        q_projected = sem("q_projected")
        q_relued = sem("q_relued")
        q_split = sem("q_split")
        selecting = sem("selecting")
        first_q_selected = sem("first_q_selected")
        first_q_spread = sem("first_q_spread")
        first_k_selected = sem("first_k_selected")
        first_k_spread = sem("first_k_spread")
        q_replicated = sem("q_replicated")
        q_masked = sem("q_masked")
        first_projected = sem("first_projected")
        first_evacuated = sem("first_evacuated")
        work_filled = sem("work_filled")
        work_free = sem("work_free")
        k_max_ready = sem("k_max_ready")
        first_k_low = sem("first_k_low")
        k_high_ready = sem("k_high_ready")
        k_cent_ready = sem("k_cent_ready")
        k_low_ready = sem("k_low_ready")
        k_replicated = sem("k_replicated")
        qbd_ready = sem("qbd_ready")
        keep_ready = sem("keep_ready")
        v_ready = sem("v_ready")
        scores_ready = sem("scores_ready")
        probs_ready = sem("probs_ready")
        pv_done = sem("pv_done")
        o_copied = sem("o_copied")
        den_read = sem("den_read")
        den_inverted = sem("den_inverted")
        o_half_normed = sem("o_half_normed")
        out_ready = sem("out_ready")
        out_stored = sem("out_stored")
        bound_made = sem("bound_made")
        kept_counted = sem("kept_counted")
        selectors_ready = sem("selectors_ready")
        checks_summed = sem("checks_summed")
        check_step = sem("check_step")
        path_chosen = sem("path_chosen")
        g_loaded = sem("g_loaded")
        g_projected = sem("g_projected")
        g_values_projected = sem("g_values_projected")
        g_prepared = sem("g_prepared")
        g_keys_made = sem("g_keys_made")
        g_query_made = sem("g_query_made")
        g_scored = sem("g_scored")
        g_masked = sem("g_masked")
        g_exped = sem("g_exped")
        g_inverted = sem("g_inverted")
        g_transposed = sem("g_transposed")
        g_copied = sem("g_copied")
        g_summed = sem("g_summed")
        g_head_done = sem("g_head_done")
        g_out_made = sem("g_out_made")
        g_stored = sem("g_stored")

        WORKS = KCHUNKS + VGROUPS

        def works_before(b):
            return 0 if isinstance(b, int) and b == 0 else (WORKS + 1) * b - 1

        def pairs_loop(eng, first, last, body):
            with nc.Fori(0, (last - first) // 2, engines=[eng.engine], hint_back_edge=True) as i:
                for k in range(2):
                    body(first + k + 2 * i, (first + k) % 2)

        def general_path(eng, body, after=lambda: None):
            eng.wait_ge(path_chosen, 1)
            passed = eng.value_load(bounded[0:1, 0:1], min_val=0, max_val=B)
            with eng.If(passed < B):
                with nc.Fori(0, B, engines=[eng.engine]) as b:
                    body(b)
                after()

        def row(ap, b):
            return ap[b] if isinstance(b, int) else ap[bass.ds(b, 1)].rearrange("a p n -> (a p) n")

        block = ctx.enter_context(nc.Block())

        @block.sync
        def _(sp):
            def load_keys(b, parity):
                sp.dma_start(keyT[:, parity, 0:SK], row(ctxT, b)).then_inc(key_loaded[parity], 16)

            def replicate(parity, source, slots):
                for t in range(QUADS):
                    for s in slots:
                        sp.dma_start(k_parts[32 * s:32 * s + 32, parity, t, 0:SK].bitcast(F32),
                                     source[32 * t:32 * t + 32, :].bitcast(F32)).then_inc(k_replicated, 16)

            def spread_keys(b, parity):
                sp.wait_ge(k_high_ready, b + 1)
                replicate(parity, k_high, (0, 2))
                sp.wait_ge(k_low_ready, b + 1)
                replicate(parity, k_low, (1, 3))

            def store(b):
                sp.wait_ge(out_ready, b + 1)
                src = out_sb[:, b, :] if isinstance(b, int) else \
                    out_sb[:, bass.ds(b, 1), :].rearrange("q a d -> q (a d)")
                sp.dma_start(row(out, b), src).then_inc(out_stored, 16)

            sp.dma_start(wk_sb[:], Wk).then_inc(wk_loaded, 16)
            for c in range(KCHUNKS):
                end = min((c + 1) * BANK, SK)
                sp.dma_start(keyT[:, 0, c * BANK:end], ctxT[0][:, c * BANK:end]
                             ).then_inc(first_keys_loaded[c], 16)
            sp.dma_start(wv_sb[:, 0:D], Wv).then_inc(wv_loaded, 16)
            sp.dma_start(bv_sb[:], bv.to_broadcast([P, D])).then_inc(wv_loaded, 16)
            load_keys(1, 1)
            sp.dma_start(x_sb[:], x.rearrange("b q d -> q b d")).then_inc(x_loaded, 16)
            for part, source, slots in ((0, q_high, (0, 1)), (1, q_low, (2, 3))):
                sp.wait_ge(q_split, 3 + part)
                for t in range(QUADS):
                    for n in slots:
                        sp.dma_start(
                            query_rep[32 * n:32 * n + 32, t, :].rearrange("p (g n) -> p g n", n=QB * SQ).bitcast(F32),
                            source[32 * t:32 * t + 32].bitcast(F32)).then_inc(q_replicated, 16)

            def batch(b, parity, more=True, before=True):
                if more:
                    if before:
                        sp.wait_ge(work_free, works_before(b))
                    else:
                        sp.wait_ge(first_evacuated, KCHUNKS + VGROUPS)
                    load_keys(b + 2, parity)
                if before:
                    sp.wait_ge(scores_ready, UNITS * b)
                else:
                    sp.wait_ge(first_q_selected, 1)
                    sp.wait_ge(q_replicated, 16 * REPLICAS)
                spread_keys(b + 1, 1 - parity)
                if before:
                    store(b - 1)

            batch(0, 0, before=False)
            pairs_loop(sp, 1, B - 3, batch)
            batch(B - 3, (B - 3) % 2)
            batch(B - 2, (B - 2) % 2, more=False)
            store(B - 2)
            store(B - 1)
            sp.wait_ge(out_stored, 16 * B)

            def general(b):
                sp.dma_start(keyT[:, 0, 0:SK], row(ctxT, b)).then_inc(g_loaded, 16)
                sp.wait_ge(g_out_made, b + 1)
                sp.dma_start(row(out, b), g_out[:]).then_inc(g_stored, 16)

            general_path(sp, general, lambda: sp.wait_ge(g_stored, 16 * B))

        @block.gpsimd
        def _(pool):
            selected = selectors[:].bitcast(F32)
            nc.gpsimd.memset(selected, 0.0).then_inc(selecting, 1)
            pool.wait_ge(selecting, 1)
            for ones_at in (selected[:, :, 0:2], selected[:, :, 4:7], selected[:, :, 8:9], selected[:, :, 10:11]):
                nc.gpsimd.memset(ones_at, 1.0).then_inc(selecting, 1)
            pool.wait_ge(selecting, 5)
            nc.gpsimd.affine_select(out=selectors[:], in_=selected, compare_op=ALU.is_equal, fill=0.0, base=0,
                                    pattern=[[-32, QUADS], [0, SELECTOR_SLOTS], [-1, 32]], channel_multiplier=1
                                    ).then_inc(selecting, 1)
            nc.gpsimd.memset(blockmask[:], 1.0).then_inc(mask_step, 1)
            pool.wait_ge(mask_step, 1)
            for s in range(SLOTS):
                part = blockmask[32 * s:32 * s + 32, :]
                nc.gpsimd.affine_select(out=part, in_=part, compare_op=ALU.is_ge, fill=0.0, base=0,
                                        pattern=[[-DH, QUAD]], channel_multiplier=1).then_inc(mask_step, 1)
            pool.wait_ge(mask_step, 1 + SLOTS)
            for s in range(SLOTS):
                part = blockmask[32 * s:32 * s + 32, :]
                nc.gpsimd.affine_select(out=part, in_=part, compare_op=ALU.is_ge, fill=0.0, base=DH - 1,
                                        pattern=[[DH, QUAD]], channel_multiplier=-1).then_inc(mask_step, 1)
            pool.wait_ge(mask_step, 1 + 2 * SLOTS)
            nc.gpsimd.memset(keyT[:, :, SK:SKP], 0.0).then_inc(pads_zeroed, 1)
            nc.gpsimd.memset(wv_sb[:, D:VW], 1.0).then_inc(pads_zeroed, 1)
            nc.gpsimd.memset(shift_sb[:], SHIFT).then_inc(consts_ready, 1)
            nc.gpsimd.memset(ident[:], 0.0).then_inc(ident_ready, 1)
            pool.wait_ge(ident_ready, 1)
            nc.gpsimd.affine_select(out=ident[:], in_=ident[:], compare_op=ALU.not_equal, fill=1.0, base=0,
                                    pattern=[[-1, P]], channel_multiplier=1).then_inc(ident_ready, 1)
            pool.wait_ge(ident_ready, 2)
            nc.gpsimd.memset(values[:, 0, :, :, PAIR * DH + 1:], 0.0).then_inc(values_zeroed, 1)
            nc.gpsimd.memset(k_parts[:, :, :, SK:SKP].bitcast(F32), 0.0).then_inc(pads_zeroed, 1)
            nc.gpsimd.memset(head_sum[:], 1.0).then_inc(selectors_ready, 1)
            pool.wait_ge(selectors_ready, 1)
            nc.gpsimd.affine_select(out=head_sum[:], in_=head_sum[:], compare_op=ALU.is_ge, fill=0.0, base=0,
                                    pattern=[[-DH, HEADS]], channel_multiplier=1).then_inc(selectors_ready, 1)
            pool.wait_ge(selectors_ready, 2)
            nc.gpsimd.affine_select(out=head_sum[:], in_=head_sum[:], compare_op=ALU.is_ge, fill=0.0,
                                    base=DH - 1, pattern=[[DH, HEADS]], channel_multiplier=-1
                                    ).then_inc(selectors_ready, 1)
            pool.wait_ge(selectors_ready, 3)
            nc.gpsimd.memset(ones[:], 1.0).then_inc(selectors_ready, 1)
            pool.wait_ge(q_projected, QGROUPS)
            nc.gpsimd.memset(values[:, 1, :, :, PAIR * DH + 1:], 0.0).then_inc(values_zeroed, 1)

        @block.scalar
        def _(act):
            act.dma_start(wq_sb[:], Wq).then_inc(wq_loaded, 16)
            act.dma_start(xT_sb[:, 0:QB * SQ].rearrange("p (b q) -> p b q", b=QB), xT[:, 0:QB, :]
                          ).then_inc(first_xT_loaded, 16)
            act.dma_start(bq_sb[:], bq).then_inc(bq_loaded, 16)
            act.dma_start(bk_sb[:], bk).then_inc(bk_loaded, 16)
            act.dma_start(xT_sb[:, QB * SQ:].rearrange("p (b q) -> p b q", q=SQ), xT[:, QB:, :]
                          ).then_inc(xT_loaded, 16)

            def relu_queries(g):
                act.wait_ge(q_projected, g + 1)
                nc.scalar.activation(queryT[:, g * QB * SQ:(g + 1) * QB * SQ], psum[:, Q_BANKS[g], 0:QB * SQ],
                                     ACT.Relu, bias=bq_sb[:]).then_inc(q_relued, 1)

            act.wait_ge(bq_loaded, 16)
            relu_queries(0)
            act.wait_ge(first_q_selected, 1)
            act.wait_ge(mask_step, 1 + 2 * SLOTS)
            for h in range(QUAD):
                nc.scalar.activation(query_bd[:, 0, :, h * SQ:(h + 1) * SQ],
                                     psum[:, Q_SPREAD_BANK, 0:QUADS * SQ].rearrange("p (t q) -> p t q", q=SQ),
                                     ACT.Copy, scale=blockmask[:, h:h + 1]).then_inc(first_q_spread, 1)
            for g in range(1, QGROUPS):
                relu_queries(g)
            for c in range(KCHUNKS):
                end = min((c + 1) * BANK, SK)
                for t in range(QUADS):
                    act.wait_ge(first_k_selected, c * QUADS + t + 1)
                    nc.scalar.activation(k_parts[:, 0, t, c * BANK:end], psum[:, K_SPREAD_BANKS[t], 0:end - c * BANK],
                                         ACT.Copy).then_inc(first_k_spread, 1)
            act.wait_ge(consts_ready, 1)

            def batch(b, parity):
                for u in range(UNITS):
                    act.wait_ge(scores_ready, UNITS * b + u + 1)
                    if not isinstance(b, int) or b > 0 or u >= PROB_SLOTS:
                        act.wait_ge(pv_done, UNITS * b + u + 1 - PROB_SLOTS)
                    nc.scalar.activation(probs[:, u % PROB_SLOTS], scores_ps[:, u % SCORE_SLOTS, :, 0:QCOLS],
                                         ACT.Exp, bias=shift_sb[:], scale=SCALE).then_inc(probs_ready, 1)

            batch(0, 0)
            pairs_loop(act, 1, B - 1, batch)
            batch(B - 1, 1)

            def general(b):
                with nc.Fori(0, HEADS, engines=[act.engine]) as h:
                    n = b * HEADS + h
                    act.wait_ge(g_masked, 4 * n + 4)
                    nc.scalar.activation(g_scores[:, 0:SK], g_scores[:, 0:SK], ACT.Exp, bias=g_stat[:, 1:2],
                                         accum_out=g_stat[:, 2:3]).then_inc(g_exped, 1)

            general_path(act, general)

        @block.tensor
        def _(pe):
            def work(index):
                if not isinstance(index, int) or index > 0:
                    pe.wait_ge(work_free, index)

            def project_keys(bank, parity, c, part, parts):
                end = min((c + 1) * BANK, SK)
                step = BANK // parts
                at, to = c * BANK + part * step, min(c * BANK + (part + 1) * step, end)
                return nc.tensor.matmul(bank[:, at - c * BANK:to - c * BANK], wk_sb[:], keyT[:, parity, at:to],
                                        start=True, stop=True)

            def project_values(bank, parity, g, n):
                kt = g * VGROUP + n
                return nc.tensor.matmul(bank[:, n * VW:(n + 1) * VW], keyT[:, parity, kt * P:(kt + 1) * P],
                                        wv_sb[:], start=True, stop=True)

            def transpose_outputs():
                for n in range(HALVES * PAIR):
                    mm = nc.tensor.transpose(work_ps[0:SQ, n * P:(n + 1) * P], o_sb[:, n * SQ:(n + 1) * SQ],
                                             ident[:])
                return mm

            def prepare(b, parity, k, piece, index):
                if k == 0 and piece == 0:
                    pe.wait_ge(key_loaded[parity], 8 * (b - parity) + 16 * parity)
                if piece == 0:
                    work(index)
                if k < KCHUNKS:
                    mm = project_keys(work_ps, parity, k, piece, KPIECES)
                else:
                    mm = project_values(work_ps, parity, k - KCHUNKS, piece)
                if piece == (KPIECES if k < KCHUNKS else VGROUP) - 1:
                    mm.then_inc(work_filled, 1)

            def scores(b, parity, u):
                kt, half = divmod(u, HALVES)
                if u == 0 and isinstance(b, int) and b == 0:
                    pe.wait_ge(first_k_spread, KCHUNKS * QUADS)
                    pe.wait_ge(first_q_spread, QUAD)
                elif u == 0:
                    pe.wait_ge(k_replicated, 16 * REPLICAS * b)
                    pe.wait_ge(qbd_ready, b)
                if not isinstance(b, int) or b > 0 or u >= SCORE_SLOTS:
                    pe.wait_ge(probs_ready, UNITS * b + u + 1 - SCORE_SLOTS)
                for n in range(HALF_QUADS):
                    t = half * HALF_QUADS + n
                    mm = nc.tensor.matmul(scores_ps[:, u % SCORE_SLOTS, n, 0:QCOLS],
                                          k_parts[:, parity, t, kt * P:(kt + 1) * P],
                                          query_bd[:, parity, t, :], start=True, stop=True)
                mm.then_inc(scores_ready, 1)

            def value_products(b, parity, u):
                kt, half = divmod(u, HALVES)
                if u == 0:
                    pe.wait_ge(v_ready, (KT + 1) * (b + 1))
                    if not isinstance(b, int) or b > 0:
                        pe.wait_ge(o_copied, b)
                pe.wait_ge(probs_ready, UNITS * b + u + 1)
                for c in range(HALF_PAIRS):
                    n, off = divmod(c * PCOLS, QCOLS)
                    mm = nc.tensor.matmul(
                        o_ps[c * VCOLS:(c + 1) * VCOLS, half * PCOLS:(half + 1) * PCOLS],
                        values[:, parity, kt, half * HALF_PAIRS + c, :],
                        probs[:, u % PROB_SLOTS, n, off:off + PCOLS],
                        start=(u == 0), stop=(kt == KT - 1), skip_group_check=True)
                mm.then_inc(pv_done, 1)

            OUTPUTS = (-1, 0)
            K, V = 0, KCHUNKS
            SIDE_WORK = (
                ((), ((K, 0), (K, 1)), (), (), ((K + 1, 0), (K + 1, 1))),
                ((), ((K + 2, 0), (K + 2, 1)), (), (), (OUTPUTS,)),
                ((), ((V, 0),), ((V, 1),), ((V, 2),), ()),
                ((), ((V + 1, 0),), ((V + 1, 1),), ((V + 1, 2),), ()),
                ((), ((V + 2, 0),), ((V + 2, 1),), ((V + 2, 2),), ()),
                ((), ((V + 3, 0),), ((V + 3, 1),), ((V + 3, 2),), ()),
            )
            GROUP = UNITS // len(SIDE_WORK)
            assert GROUP * len(SIDE_WORK) == UNITS and GROUP <= PROB_SLOTS and GROUP + 1 == len(SIDE_WORK[0])

            def batch(b, parity, first=False, last=False):
                used = works_before(b)

                def side_work(steps):
                    nonlocal used
                    for step in steps:
                        k, piece = step
                        if step == OUTPUTS:
                            if not first:
                                work(used)
                                pe.wait_ge(o_copied, b)
                                transpose_outputs().then_inc(work_filled, 1)
                                used = used + 1
                        elif not last:
                            prepare(b + 1, 1 - parity, k, piece, used)
                            if piece == (KPIECES if k < KCHUNKS else VGROUP) - 1:
                                used = used + 1

                for group, places in enumerate(SIDE_WORK):
                    side_work(places[0])
                    for n in range(GROUP):
                        u = group * GROUP + n
                        if u + LEAD < UNITS:
                            scores(b, parity, u + LEAD)
                        elif not last:
                            scores(b + 1, 1 - parity, u + LEAD - UNITS)
                        side_work(places[1 + n])
                    if last and group == len(SIDE_WORK) // 2:
                        check_batches(used)
                    for n in range(GROUP):
                        value_products(b, parity, group * GROUP + n)
                return used

            def check_batches(used):
                pe.wait_ge(selectors_ready, 4)
                work(used)
                pe.wait_ge(bound_made, B)
                nc.tensor.matmul(work_ps[0:B, 0:HEADS], bound_terms[:], head_sum[:], start=True, stop=True)
                pe.wait_ge(kept_counted, B)
                nc.tensor.matmul(work_ps[0:B, HEADS:HEADS + 1], kept_keys[:], ones[:, 0:1],
                                 start=True, stop=True).then_inc(checks_summed, 1)
                pe.wait_ge(check_step, 4)
                nc.tensor.matmul(work_ps[0:1, 0:1], batch_checks[:, 3:4], ones[0:B, 0:1],
                                 start=True, stop=True).then_inc(checks_summed, 1)

            def project_queries(g):
                nc.tensor.matmul(psum[:, Q_BANKS[g], 0:QB * SQ], wq_sb[:], xT_sb[:, g * QB * SQ:(g + 1) * QB * SQ],
                                 start=True, stop=True).then_inc(q_projected, 1)

            def select(bank, t, high, low, high_at, low_at):
                nc.tensor.matmul(bank, selectors[:, t, high_at:high_at + SLOTS, :], high, start=True, stop=False)
                return nc.tensor.matmul(bank, selectors[:, t, low_at:low_at + SLOTS, :], low, start=False, stop=True)

            pe.wait_ge(wq_loaded, 16)
            pe.wait_ge(first_xT_loaded, 16)
            project_queries(0)
            pe.wait_ge(wk_loaded, 16)
            for c in range(KCHUNKS):
                pe.wait_ge(first_keys_loaded[c], 16)
                project_keys(psum[:, K_BANKS[c], :], 0, c, 0, 1).then_inc(first_projected, 1)
            pe.wait_ge(selecting, 6)
            pe.wait_ge(q_split, 2)
            for t in range(QUADS):
                mm = select(psum[:, Q_SPREAD_BANK, t * SQ:(t + 1) * SQ], t, q_high[:, 0, 0:SQ], q_low[:, 0, 0:SQ],
                            Q_HIGH_AT, Q_LOW_AT)
            mm.then_inc(first_q_selected, 1)
            pe.wait_ge(xT_loaded, 16)
            for g in range(1, QGROUPS):
                project_queries(g)
            pe.wait_ge(wv_loaded, 32)
            pe.wait_ge(pads_zeroed, 2)
            pe.wait_ge(q_relued, 1)
            for g in range(VGROUPS):
                if g < KCHUNKS:
                    pe.wait_ge(first_evacuated, g + 1)
                for n in range(VGROUP):
                    mm = project_values(psum[:, V_BANKS[g], :], 0, g, n)
                mm.then_inc(first_projected, 1)
            pe.wait_ge(first_q_spread, QUAD)
            pe.wait_ge(q_relued, QGROUPS)
            for c in range(KCHUNKS):
                end = min((c + 1) * BANK, SK)
                if c < KCHUNKS - 1:
                    pe.wait_ge(first_k_low, c + 1)
                else:
                    pe.wait_ge(k_low_ready, 1)
                for t in range(QUADS):
                    if c > 0:
                        pe.wait_ge(first_k_spread, (c - 1) * QUADS + t + 1)
                    select(psum[:, K_SPREAD_BANKS[t], 0:end - c * BANK], t, k_high[:, c * BANK:end],
                           k_low[:, c * BANK:end], K_HIGH_AT, K_LOW_AT).then_inc(first_k_selected, 1)
            pe.wait_ge(first_evacuated, KCHUNKS + VGROUPS)
            pe.wait_ge(pads_zeroed, 3)
            pe.wait_ge(ident_ready, 2)
            for u in range(LEAD):
                scores(0, 0, u)
            batch(0, 0, first=True)
            pairs_loop(pe, 1, B - 1, batch)
            used = batch(B - 1, 1, last=True)
            pe.wait_ge(path_chosen, 1)
            pe.wait_ge(o_copied, B)
            transpose_outputs().then_inc(work_filled, 1)

            def general(b):
                pe.wait_ge(g_loaded, 16 * (b + 1))
                for c in range(KCHUNKS):
                    nc.tensor.matmul(psum[:, c, :], wk_sb[:], keyT[:, 0, c * BANK:(c + 1) * BANK],
                                     start=True, stop=True)
                    nc.tensor.matmul(psum[:, KCHUNKS + c, :], ones[:], keyT[:, 0, c * BANK:(c + 1) * BANK],
                                     start=True, stop=True).then_inc(g_projected, 1)
                pe.wait_ge(g_keys_made, 3 * (b + 1))
                for kt in range(KT):
                    c, n = divmod(kt, BANK // P)
                    nc.tensor.matmul(psum[:, c, n * P:(n + 1) * P], keyT[:, 0, kt * P:(kt + 1) * P],
                                     wv_sb[:, 0:D], start=True, stop=True).then_inc(g_values_projected, 1)
                with nc.Fori(0, HEADS, engines=[pe.engine]) as h:
                    n = b * HEADS + h
                    pe.wait_ge(g_prepared, 2 * (b + 1))
                    pe.wait_ge(g_query_made, n + 1)
                    for c in range(KCHUNKS):
                        mm = nc.tensor.matmul(psum[0:SQ, c, :], g_query, g_keys[:, c * BANK:(c + 1) * BANK],
                                              start=True, stop=True)
                    mm.then_inc(g_scored, 1)
                    pe.wait_ge(g_exped, n + 1)
                    for kt in range(KT):
                        c, m = divmod(kt, BANK // P)
                        mm = nc.tensor.transpose(psum[:, KCHUNKS + c, m * P:m * P + SQ],
                                                 g_scores[:, kt * P:(kt + 1) * P], ident[0:SQ, 0:SQ])
                    mm.then_inc(g_transposed, 1)
                    pe.wait_ge(g_copied, n + 1)
                    for kt in range(KT):
                        mm = nc.tensor.matmul(work_ps[0:SQ, 0:DH], g_probsT[:, kt, 0:SQ],
                                              g_values[:, kt, bass.ds(h * DH, DH)],
                                              start=(kt == 0), stop=(kt == KT - 1))
                    mm.then_inc(g_summed, 1)

            general_path(pe, general)

        @block.vector
        def _(dve):
            v = nc.vector
            def read_keys(b, k0, before=True):
                for c in range(KCHUNKS):
                    end = min((c + 1) * BANK, SK)
                    filled, free, bank = (work_filled, work_free, work_ps) if before else \
                        (first_projected, first_evacuated, psum[:, K_BANKS[c], :])
                    dve.wait_ge(filled, k0 + c + 1)
                    if c == 0 and before:
                        dve.wait_ge(k_high_ready, b)
                        dve.wait_ge(k_cent_ready, b)
                    v.tensor_scalar(k_raw[:, c * BANK:end], bank[:, 0:end - c * BANK], bk_sb[:], None,
                                    ALU.add, ALU.max, accum_out=k_chunk_max[:, c:c + 1]).then_inc(free, 1)

            def max_keys(b, parity, k0, before=True):
                dve.wait_ge(work_free if before else first_evacuated, k0 + KCHUNKS)
                v.tensor_reduce(k_max[:, parity:parity + 1], k_chunk_max[:], AX.X, ALU.max).then_inc(k_max_ready, 1)
                dve.wait_ge(k_max_ready, 2 * b + 1)
                v.tensor_scalar(k_max[:, parity:parity + 1], k_max[:, parity:parity + 1], 0.0, None, ALU.max
                                ).then_inc(k_max_ready, 1)
                dve.wait_ge(k_max_ready, 2 * b + 2)

            def center_keys(target, parity, done):
                v.tensor_scalar(target[:, 0:SK], k_raw[:, 0:SK], 0.0, k_max[:, parity:parity + 1], ALU.max, ALU.subtract
                                ).then_inc(done, 1)

            def low_keys(done, at=slice(0, SK)):
                v.tensor_tensor(k_low[:, at], k_cent[:, at], k_high[:, at].bitcast(F32), ALU.subtract
                                ).then_inc(done, 1)

            def bound_scores(b, parity):
                at = slice(b, b + 1) if isinstance(b, int) else bass.ds(b, 1)
                v.tensor_tensor(bound_terms[:, at], k_max[:, parity:parity + 1], q_max[:, at], ALU.mult
                                ).then_inc(bound_made, 1)

            def finish_values(b, parity, g, index, before=True):
                rows = slice(g * VGROUP, (g + 1) * VGROUP)
                filled, free, bank = (work_filled, work_free, work_ps) if before else \
                    (first_projected, first_evacuated, psum[:, V_BANKS[g], :])
                dve.wait_ge(filled, index + 1)
                work = bank[:, 0:VGROUP * VW].rearrange("p (n w) -> p n w", w=VW)
                v.tensor_scalar(keep[:, rows], work[:, :, D], 0.0, None, ALU.not_equal).then_inc(keep_ready, 1)
                v.tensor_tensor(v_biased[:, g % 2], work[:, :, 0:D],
                                bv_sb[:].unsqueeze(1).to_broadcast([P, VGROUP, D]), ALU.add
                                ).then_inc(free, 1)
                dve.wait_ge(keep_ready, VGROUPS * b + g + 1)
                dve.wait_ge(free, index + 1)
                for n in range(VGROUP):
                    kt = g * VGROUP + n
                    v.tensor_scalar(values[:, parity, kt, :, 0:PAIR * DH],
                                    v_biased[:, g % 2, n].rearrange("p (a w) -> p a w", w=PAIR * DH),
                                    0.0, keep[:, kt:kt + 1], ALU.max, ALU.mult).then_inc(v_ready, 1)

            def finish_keep(b, parity):
                v.tensor_copy(values[:, parity, :, :, PAIR * DH],
                              keep[:].unsqueeze(2).to_broadcast([P, KT, PAIRS])).then_inc(v_ready, 1)
                at = slice(b, b + 1) if isinstance(b, int) else bass.ds(b, 1)
                v.tensor_reduce(kept_keys[:, at], keep[:], AX.X, ALU.add).then_inc(kept_counted, 1)

            def spread_queries(b, parity):
                src = query_rep[:, :, b * SQ:(b + 1) * SQ] if isinstance(b, int) else \
                    query_rep[:, :, bass.ds(b * SQ, SQ)]
                for t in range(QUADS):
                    ins = v.tensor_tensor(
                        query_bd[:, parity, t, :].rearrange("p (h q) -> p h q", h=QUAD),
                        src[:, t].bitcast(F32).unsqueeze(1).to_broadcast([P, QUAD, SQ]),
                        blockmask[:].unsqueeze(2).to_broadcast([P, QUAD, SQ]), ALU.mult)
                ins.then_inc(qbd_ready, 1)

            def copy_outputs(b):
                dve.wait_ge(pv_done, UNITS * (b + 1))
                v.tensor_copy(o_sb[:], o_ps[:, 0:HALVES * PCOLS]).then_inc(o_copied, 1)

            def finish_outputs(b, index):
                dve.wait_ge(work_filled, index + 1)
                t = work_ps[0:SQ, :].rearrange("q (rj c w) -> q rj c w", c=HALF_PAIRS, w=VCOLS)
                v.tensor_scalar(inv_den[:], t[:, :, :, PAIR * DH], DEN_FLOOR, None, ALU.max).then_inc(den_read, 1)
                dve.wait_ge(den_read, b + 1)
                v.reciprocal(inv_den[:], inv_den[:]).then_inc(den_inverted, 1)
                dve.wait_ge(den_inverted, b + 1)
                o = o_norm[:].rearrange("q (r c j d) -> q r c j d", r=HALVES, c=HALF_PAIRS, j=PAIR)
                t = work_ps[0:SQ, :].rearrange("q (r j c w) -> q r j c w", r=HALVES, j=PAIR, w=VCOLS)
                i = inv_den[:].rearrange("q (r j) c -> q r j c", j=PAIR)
                for j, done in ((0, o_half_normed), (1, work_free)):
                    v.tensor_tensor(o[:, :, :, j, :], t[:, :, j, :, j * DH:(j + 1) * DH],
                                    i[:, :, j, :].unsqueeze(3).to_broadcast([SQ, HALVES, HALF_PAIRS, DH]),
                                    ALU.mult).then_inc(done, 1)
                dve.wait_ge(o_half_normed, b + 1)
                dve.wait_ge(work_free, index + 1)
                at = slice(b, b + 1) if isinstance(b, int) else bass.ds(b, 1)
                v.scalar_tensor_tensor(out=out_sb[:, at, :].rearrange("q a d -> q (a d)"), in0=o_norm[:],
                                       scalar=q_mask[:, at], in1=x_sb[:, at, :].rearrange("q a d -> q (a d)"),
                                       op0=ALU.mult, op1=ALU.add).then_inc(out_ready, 1)

            def batch(b, parity, first=False, last=False):
                used = works_before(b)
                if not first:
                    copy_outputs(b - 1)
                if not last:
                    read_keys(b + 1, used)
                    max_keys(b + 1, 1 - parity, used)
                    if first:
                        dve.wait_ge(first_k_selected, KCHUNKS * QUADS)
                    else:
                        dve.wait_ge(k_replicated, 16 * REPLICAS * b)
                    center_keys(k_high, 1 - parity, k_high_ready)
                    used = used + KCHUNKS
                if not first:
                    finish_outputs(b - 1, used)
                    used = used + 1
                if not last:
                    center_keys(k_cent, 1 - parity, k_cent_ready)
                    if first:
                        dve.wait_ge(values_zeroed, 2)
                    finish_values(b + 1, 1 - parity, 0, used)
                    dve.wait_ge(k_high_ready, b + 2)
                    dve.wait_ge(k_cent_ready, b + 2)
                    low_keys(k_low_ready)
                    finish_values(b + 1, 1 - parity, 1, used + 1)
                    if first:
                        dve.wait_ge(mask_step, 1 + 2 * SLOTS)
                        dve.wait_ge(q_replicated, 16 * REPLICAS)
                    spread_queries(b + 1, 1 - parity)
                    for g in range(2, VGROUPS):
                        finish_values(b + 1, 1 - parity, g, used + g)
                    if first:
                        reduce_queries()
                        bound_scores(b, parity)
                    bound_scores(b + 1, 1 - parity)
                    finish_keep(b + 1, 1 - parity)
                    used = used + VGROUPS
                return used

            def reduce_queries():
                dve.wait_ge(x_loaded, 16)
                v.tensor_reduce(q_sum[:], x_sb[:], AX.X, ALU.add).then_inc(q_masked, 1)
                dve.wait_ge(q_masked, 1)
                v.tensor_scalar(q_mask[:], q_sum[:], 0.0, None, ALU.not_equal).then_inc(q_masked, 1)
                v.tensor_reduce(q_max[:], queryT[:].rearrange("p (b q) -> p b q", b=B), AX.X, ALU.max
                                ).then_inc(q_masked, 1)
                dve.wait_ge(q_masked, 3)

            def split_queries(first, last):
                dve.wait_ge(q_relued, last)
                relued = queryT[:, first * QB * SQ:last * QB * SQ].rearrange("p (g n) -> p g n", n=QB * SQ)
                part = 1 if first == 0 else 3
                v.tensor_copy(q_high[:, first:last, :], relued).then_inc(q_split, 1)
                dve.wait_ge(q_split, part)
                v.tensor_tensor(q_low[:, first:last, :], relued, q_high[:, first:last, :].bitcast(F32),
                                ALU.subtract).then_inc(q_split, 1)

            split_queries(0, 1)
            dve.wait_ge(bk_loaded, 16)
            read_keys(0, 0, False)
            max_keys(0, 0, 0, False)
            center_keys(k_high, 0, k_high_ready)
            center_keys(k_cent, 0, k_cent_ready)
            dve.wait_ge(k_high_ready, 1)
            dve.wait_ge(k_cent_ready, 1)
            for c in range(KCHUNKS):
                low_keys(first_k_low if c < KCHUNKS - 1 else k_low_ready, slice(c * BANK, min((c + 1) * BANK, SK)))
            split_queries(1, QGROUPS)
            dve.wait_ge(wv_loaded, 32)
            dve.wait_ge(values_zeroed, 1)
            for g in range(VGROUPS):
                finish_values(0, 0, g, KCHUNKS + g, False)
            finish_keep(0, 0)
            batch(0, 0, first=True)
            pairs_loop(dve, 1, B - 1, batch)
            used = batch(B - 1, 1, last=True)

            dve.wait_ge(checks_summed, 1)
            v.tensor_reduce(batch_checks[:, 0:1], work_ps[0:B, 0:HEADS], AX.X, ALU.max).then_inc(check_step, 1)
            v.tensor_scalar(batch_checks[:, 2:3], work_ps[0:B, HEADS:HEADS + 1], 0.5, None, ALU.is_ge
                            ).then_inc(check_step, 1)
            dve.wait_ge(check_step, 2)
            v.tensor_scalar(batch_checks[:, 1:2], batch_checks[:, 0:1], BOUND_LIMIT / SCALE, None, ALU.is_le
                            ).then_inc(check_step, 1)
            dve.wait_ge(check_step, 3)
            v.tensor_tensor(batch_checks[:, 3:4], batch_checks[:, 1:2], batch_checks[:, 2:3], ALU.mult
                            ).then_inc(check_step, 1)
            dve.wait_ge(checks_summed, 2)
            v.tensor_copy(bounded[:], work_ps[0:1, 0:1]).then_inc(path_chosen, 1)
            copy_outputs(B - 1)
            finish_outputs(B - 1, used)

            def flat(ap, parts=P):
                return ap.rearrange("p (c n) -> p c n", n=BANK)

            def general(b):
                at = bass.ds(b, 1)
                dve.wait_ge(g_projected, KCHUNKS * (b + 1))
                v.tensor_scalar(flat(g_keys[:]), psum[:, 0:KCHUNKS, :], bk_sb[:], 0.0, ALU.add, ALU.max
                                ).then_inc(g_keys_made, 1)
                v.tensor_scalar(flat(g_keep[:]), psum[:, KCHUNKS:2 * KCHUNKS, :], 0.0, None, ALU.not_equal
                                ).then_inc(g_keys_made, 1)
                dve.wait_ge(g_keys_made, 3 * b + 2)
                v.tensor_scalar(g_mask, g_keep[:], -1.0, NEG, ALU.add, ALU.mult).then_inc(g_keys_made, 1)
                dve.wait_ge(g_values_projected, KT * (b + 1))
                for c in range(KCHUNKS):
                    n = BANK // P
                    ins = v.tensor_tensor(g_values[:, c * n:(c + 1) * n, :],
                                          psum[:, c, :].rearrange("p (n w) -> p n w", w=D),
                                          bv_sb[:].unsqueeze(1).to_broadcast([P, n, D]), ALU.add)
                ins.then_inc(g_prepared, 1)
                dve.wait_ge(g_prepared, 2 * b + 1)
                v.tensor_scalar(g_values, g_values, 0.0, None, ALU.max).then_inc(g_prepared, 1)
                with nc.Fori(0, HEADS, engines=[dve.engine]) as h:
                    n = b * HEADS + h
                    dve.wait_ge(g_keys_made, 3 * (b + 1))
                    v.tensor_scalar(g_query, queryT[:, bass.ds(b * SQ, SQ)], head_sum[:, bass.ds(h, 1)], None,
                                    ALU.mult).then_inc(g_query_made, 1)
                    dve.wait_ge(g_scored, n + 1)
                    v.scalar_tensor_tensor(out=flat(g_scores, SQ), in0=psum[0:SQ, 0:KCHUNKS, :], scalar=SCALE,
                                           in1=flat(g_keep[0:SQ, :]), op0=ALU.mult, op1=ALU.mult
                                           ).then_inc(g_masked, 1)
                    dve.wait_ge(g_masked, 4 * n + 1)
                    v.tensor_tensor(g_scores, g_scores, g_mask[0:SQ], ALU.add).then_inc(g_masked, 1)
                    dve.wait_ge(g_masked, 4 * n + 2)
                    v.tensor_reduce(g_stat[:, 0:1], g_scores[:, 0:SK], AX.X, ALU.max).then_inc(g_masked, 1)
                    dve.wait_ge(g_masked, 4 * n + 3)
                    v.memset(g_scores[:, SK:SKP], 0.0)
                    v.tensor_scalar(g_stat[:, 1:2], g_stat[:, 0:1], -1.0, None, ALU.mult).then_inc(g_masked, 1)
                    dve.wait_ge(g_exped, n + 1)
                    v.reciprocal(g_stat[:, 3:4], g_stat[:, 2:3]).then_inc(g_inverted, 1)
                    dve.wait_ge(g_transposed, n + 1)
                    for c in range(KCHUNKS):
                        m = BANK // P
                        ins = v.tensor_copy(g_probsT[:, c * m:(c + 1) * m, 0:SQ],
                                            psum[:, KCHUNKS + c, :].rearrange("p (n q) -> p n q", q=P)[:, :, 0:SQ])
                    ins.then_inc(g_copied, 1)
                    dve.wait_ge(g_summed, n + 1)
                    dve.wait_ge(g_inverted, n + 1)
                    v.tensor_scalar(g_out[:, bass.ds(h * DH, DH)], work_ps[0:SQ, 0:DH], g_stat[:, 3:4], None,
                                    ALU.mult).then_inc(g_head_done, 1)
                dve.wait_ge(g_head_done, HEADS * (b + 1))
                v.scalar_tensor_tensor(out=g_out[:], in0=g_out[:], scalar=q_mask[:, at],
                                       in1=x_sb[:, at, :].rearrange("q a d -> q (a d)"),
                                       op0=ALU.mult, op1=ALU.add).then_inc(g_out_made, 1)
                dve.wait_ge(g_stored, 16 * (b + 1))

            general_path(dve, general)


def kernel(**inputs):
    import numpy as np
    import concourse.bacc as bacc
    from concourse.bass_utils import run_bass_kernel_spmd

    a = {name: np.asarray(value) for name, value in inputs.items()}
    arrays = {
        "x": a["x"],
        "xT": np.ascontiguousarray(a["x"].transpose(2, 0, 1)),
        "ctxT": np.ascontiguousarray(a["ctx_1024"].transpose(0, 2, 1)),
        "Wq": a["L0_xattn_Wq"],
        "bq": a["L0_xattn_bq"].reshape(-1, 1),
        "Wk": a["L0_xattn_Wk"],
        "bk": a["L0_xattn_bk"].reshape(-1, 1),
        "Wv": a["L0_xattn_Wv"],
        "bv": a["L0_xattn_bv"].reshape(1, -1),
    }
    nc = bacc.Bacc("TRN2", target_bir_lowering=False, num_devices=1)
    args = [nc.dram_tensor(f"in_{name}", value.shape, mybir.dt.from_np(value.dtype), kind="ExternalInput").ap()
            for name, value in arrays.items()]
    args.append(nc.dram_tensor("out", a["x"].shape, F32, kind="ExternalOutput").ap())
    attention(nc, *args)
    r = run_bass_kernel_spmd(nc, [{f"in_{name}": value for name, value in arrays.items()}], core_ids=[0])
    return r.results[0]["out"]
```
